# Optimizing a Trainium2 kernel written in Bass

```python
import numpy as np
import jax
import jax.numpy as jnp

def _softmax(x, axis=-1):
    return jax.nn.softmax(x, axis=axis)

def _gelu(x):
    return jax.nn.gelu(x, approximate=True)

def _silu(x):
    return jax.nn.silu(x)

def _sigmoid(x):
    return jax.nn.sigmoid(x)

def _layernorm(x, axis=-1, eps=1e-05):
    m = jnp.mean(x, axis=axis, keepdims=True)
    v = jnp.var(x, axis=axis, keepdims=True)
    return (x - m) / jnp.sqrt(v + eps)

def _scatter_add(tgt, idx, src, axis=0):
    return tgt.at[idx].add(src)

def _segment_sum(src, seg, n):
    return jax.ops.segment_sum(src, seg, n)
kernel_name = 'mk_sandwich_d1_jaxref_r8_cc53a6'

def setup_inputs(seed: int=0):
    np.random.seed(seed)
    _w = jnp.asarray

    def _L0_attn_setup():
        import jax, jax.numpy as jnp
        import numpy as np
        D_MODEL = 256
        D_STATE = 16
        D_CONV = 4
        EXPAND = 2
        H = 16
        D_INNER = D_MODEL * EXPAND
        D_HEAD = D_INNER // H
        TOTAL = 2 * D_INNER + H + 2 * H * D_STATE
        BATCH = 4
        SEQ = 512
        EPS = 1.1920929e-07

        def _forward(x, w_norm, W_in, w_conv, dt_bias, A_log, W_h2i, W_out):
            b, l, _ = x.shape
            residual = x
            xn = x * jax.lax.rsqrt(jnp.mean(x * x, axis=-1, keepdims=True) + EPS) * w_norm
            proj = jnp.einsum('bld,td->blt', xn, W_in)
            z = proj[..., :D_INNER]
            xi = proj[..., D_INNER:2 * D_INNER]
            dt = proj[..., 2 * D_INNER:2 * D_INNER + H]
            o = 2 * D_INNER + H
            Bm = proj[..., o:o + H * D_STATE].reshape(b, l, H, D_STATE)
            Cm = proj[..., o + H * D_STATE:].reshape(b, l, H, D_STATE)
            xc = jax.lax.conv_general_dilated(xi.transpose(0, 2, 1), w_conv, window_strides=(1,), padding=[(D_CONV - 1, 0)], feature_group_count=D_INNER)
            xi = jax.nn.silu(xc.transpose(0, 2, 1))
            dt = jax.nn.softplus(dt + dt_bias)
            A = -jnp.exp(A_log)
            dA = jnp.exp(dt * A)
            x_mean = xi.reshape(b, l, H, D_HEAD).mean(axis=-1)
            u = (dt * x_mean)[..., None] * Bm
            h0 = jnp.zeros((b, H, D_STATE), xi.dtype)

            def step(h, inp):
                dA_t, u_t, C_t = inp
                h = dA_t[..., None] * h + u_t
                y_t = jnp.sum(h * C_t, axis=-1)
                return (h, y_t)
            _, ys = jax.lax.scan(step, h0, (dA.transpose(1, 0, 2), u.transpose(1, 0, 2, 3), Cm.transpose(1, 0, 2, 3)))
            y = ys.transpose(1, 0, 2)
            y = jnp.einsum('blh,ih->bli', y, W_h2i)
            y = y * jax.nn.silu(z)
            out = jnp.einsum('bli,di->bld', y, W_out) + residual
            return out
        key = jax.random.key(seed)
        ks = jax.random.split(key, 6)
        s = 0.02
        return {'x': jax.random.normal(ks[0], (BATCH, SEQ, D_MODEL), jnp.float32), 'w_norm': jnp.ones((D_MODEL,), jnp.float32), 'W_in': jax.random.normal(ks[1], (TOTAL, D_MODEL), jnp.float32) * s, 'w_conv': jax.random.normal(ks[2], (D_INNER, 1, D_CONV), jnp.float32) * 0.2, 'dt_bias': jax.random.normal(ks[3], (H,), jnp.float32), 'A_log': jnp.log(0.001 + jnp.arange(1, H + 1, dtype=jnp.float32)), 'W_h2i': jax.random.normal(ks[4], (D_INNER, H), jnp.float32) * s, 'W_out': jax.random.normal(ks[5], (D_MODEL, D_INNER), jnp.float32) * s}
    _L0_attn_in = _L0_attn_setup()

    def _L0_ffn_setup():
        import jax, jax.numpy as jnp
        import numpy as np
        E = 64
        K = 6
        NG = 8
        TKG = 4
        SCALE = 2.5
        CAP = 64

        def _router(x, gate_w, e_bias):
            logits = x.astype(jnp.float32) @ gate_w.T
            scores = jax.nn.sigmoid(logits)
            sc = scores + e_bias[None, :]
            T = x.shape[0]
            gs = sc.reshape(T, NG, E // NG)
            grp_score = jax.lax.top_k(gs, 2)[0].sum(-1)
            _, gidx = jax.lax.top_k(grp_score, TKG)
            gmask = jax.nn.one_hot(gidx, NG, dtype=sc.dtype).sum(1)
            emask = jnp.repeat(gmask, E // NG, axis=1)
            masked = jnp.where(emask > 0, sc, -jnp.inf)
            _, idx = jax.lax.top_k(masked, K)
            w = jnp.take_along_axis(scores, idx, axis=1)
            w = w / (w.sum(-1, keepdims=True) + 1e-20) * SCALE
            return (idx, w)

        def _relu2(h):
            return jnp.square(jax.nn.relu(h))

        def _moe(x, idx, w, w1, w2):
            T, D = x.shape
            e_flat = idx.reshape(-1)
            tok = jnp.repeat(jnp.arange(T), K)
            oh = jax.nn.one_hot(e_flat, E, dtype=jnp.float32)
            pos = jnp.cumsum(oh, axis=0) - oh
            pos = (pos * oh).sum(-1).astype(jnp.int32)
            keep = pos < CAP
            slot = jnp.where(keep, pos, CAP)
            xd = jnp.zeros((E, CAP + 1, D), x.dtype).at[e_flat, slot].set(x[tok])
            h = _relu2(jnp.einsum('ecd,eid->eci', xd, w1))
            yd = jnp.einsum('eci,edi->ecd', h, w2)
            gate = w.reshape(-1)[:, None] * keep[:, None].astype(x.dtype)
            y_assign = yd[e_flat, slot] * gate
            return jnp.zeros((T, D), x.dtype).at[tok].add(y_assign)
        key = jax.random.key(seed)
        ks = jax.random.split(key, 6)
        D, I, SH, T = (256, 128, 512, 256)
        x = jax.random.normal(ks[0], (1, T, D), jnp.float32)
        gate_w = jax.random.normal(ks[1], (E, D), jnp.float32) * D ** (-0.5)
        e_bias = jnp.zeros((E,), jnp.float32)
        w1 = jax.random.normal(ks[2], (E, I, D), jnp.float32) * D ** (-0.5)
        w2 = jax.random.normal(ks[3], (E, D, I), jnp.float32) * I ** (-0.5)
        su = jax.random.normal(ks[4], (SH, D), jnp.float32) * D ** (-0.5)
        sd = jax.random.normal(ks[5], (D, SH), jnp.float32) * SH ** (-0.5)
        return {'hidden_states': x, 'gate_w': gate_w, 'e_bias': e_bias, 'w1': w1, 'w2': w2, 'shared_up_w': su, 'shared_down_w': sd}
    _L0_ffn_in = _L0_ffn_setup()
    _d = {'L0_attn_x': _L0_attn_in['x'], 'L0_attn_w_norm': _L0_attn_in['w_norm'], 'L0_attn_W_in': _L0_attn_in['W_in'], 'L0_attn_w_conv': _L0_attn_in['w_conv'], 'L0_attn_dt_bias': _L0_attn_in['dt_bias'], 'L0_attn_A_log': _L0_attn_in['A_log'], 'L0_attn_W_h2i': _L0_attn_in['W_h2i'], 'L0_attn_W_out': _L0_attn_in['W_out'], 'L0_ffn_gate_w': _L0_ffn_in['gate_w'], 'L0_ffn_e_bias': _L0_ffn_in['e_bias'], 'L0_ffn_w1': _L0_ffn_in['w1'], 'L0_ffn_w2': _L0_ffn_in['w2'], 'L0_ffn_shared_up_w': _L0_ffn_in['shared_up_w'], 'L0_ffn_shared_down_w': _L0_ffn_in['shared_down_w']}
    _x0 = _d['L0_attn_x']
    _d['L0_attn_x'] = jax.random.normal(jax.random.fold_in(jax.random.key(seed), 1), (1, 1024, 256), dtype=_x0.dtype)
    del _x0
    return _d

def reference(L0_attn_x, L0_attn_w_norm, L0_attn_W_in, L0_attn_w_conv, L0_attn_dt_bias, L0_attn_A_log, L0_attn_W_h2i, L0_attn_W_out, L0_ffn_gate_w, L0_ffn_e_bias, L0_ffn_w1, L0_ffn_w2, L0_ffn_shared_up_w, L0_ffn_shared_down_w):

    def _L0_attn_ref(x, w_norm, W_in, w_conv, dt_bias, A_log, W_h2i, W_out):
        import jax, jax.numpy as jnp
        import numpy as np
        D_MODEL = 256
        D_STATE = 16
        D_CONV = 4
        EXPAND = 2
        H = 16
        D_INNER = D_MODEL * EXPAND
        D_HEAD = D_INNER // H
        TOTAL = 2 * D_INNER + H + 2 * H * D_STATE
        BATCH = 4
        SEQ = 512
        EPS = 1.1920929e-07

        def _forward(x, w_norm, W_in, w_conv, dt_bias, A_log, W_h2i, W_out):
            b, l, _ = x.shape
            residual = x
            xn = x * jax.lax.rsqrt(jnp.mean(x * x, axis=-1, keepdims=True) + EPS) * w_norm
            proj = jnp.einsum('bld,td->blt', xn, W_in)
            z = proj[..., :D_INNER]
            xi = proj[..., D_INNER:2 * D_INNER]
            dt = proj[..., 2 * D_INNER:2 * D_INNER + H]
            o = 2 * D_INNER + H
            Bm = proj[..., o:o + H * D_STATE].reshape(b, l, H, D_STATE)
            Cm = proj[..., o + H * D_STATE:].reshape(b, l, H, D_STATE)
            xc = jax.lax.conv_general_dilated(xi.transpose(0, 2, 1), w_conv, window_strides=(1,), padding=[(D_CONV - 1, 0)], feature_group_count=D_INNER)
            xi = jax.nn.silu(xc.transpose(0, 2, 1))
            dt = jax.nn.softplus(dt + dt_bias)
            A = -jnp.exp(A_log)
            dA = jnp.exp(dt * A)
            x_mean = xi.reshape(b, l, H, D_HEAD).mean(axis=-1)
            u = (dt * x_mean)[..., None] * Bm
            h0 = jnp.zeros((b, H, D_STATE), xi.dtype)

            def step(h, inp):
                dA_t, u_t, C_t = inp
                h = dA_t[..., None] * h + u_t
                y_t = jnp.sum(h * C_t, axis=-1)
                return (h, y_t)
            _, ys = jax.lax.scan(step, h0, (dA.transpose(1, 0, 2), u.transpose(1, 0, 2, 3), Cm.transpose(1, 0, 2, 3)))
            y = ys.transpose(1, 0, 2)
            y = jnp.einsum('blh,ih->bli', y, W_h2i)
            y = y * jax.nn.silu(z)
            out = jnp.einsum('bli,di->bld', y, W_out) + residual
            return out
        return _forward(x, w_norm, W_in, w_conv, dt_bias, A_log, W_h2i, W_out)

    def _L0_ffn_ref(hidden_states, gate_w, e_bias, w1, w2, shared_up_w, shared_down_w):
        import jax, jax.numpy as jnp
        import numpy as np
        E = 64
        K = 6
        NG = 8
        TKG = 4
        SCALE = 2.5
        CAP = 64

        def _router(x, gate_w, e_bias):
            logits = x.astype(jnp.float32) @ gate_w.T
            scores = jax.nn.sigmoid(logits)
            sc = scores + e_bias[None, :]
            T = x.shape[0]
            gs = sc.reshape(T, NG, E // NG)
            grp_score = jax.lax.top_k(gs, 2)[0].sum(-1)
            _, gidx = jax.lax.top_k(grp_score, TKG)
            gmask = jax.nn.one_hot(gidx, NG, dtype=sc.dtype).sum(1)
            emask = jnp.repeat(gmask, E // NG, axis=1)
            masked = jnp.where(emask > 0, sc, -jnp.inf)
            _, idx = jax.lax.top_k(masked, K)
            w = jnp.take_along_axis(scores, idx, axis=1)
            w = w / (w.sum(-1, keepdims=True) + 1e-20) * SCALE
            return (idx, w)

        def _relu2(h):
            return jnp.square(jax.nn.relu(h))

        def _moe(x, idx, w, w1, w2):
            T, D = x.shape
            e_flat = idx.reshape(-1)
            tok = jnp.repeat(jnp.arange(T), K)
            oh = jax.nn.one_hot(e_flat, E, dtype=jnp.float32)
            pos = jnp.cumsum(oh, axis=0) - oh
            pos = (pos * oh).sum(-1).astype(jnp.int32)
            keep = pos < CAP
            slot = jnp.where(keep, pos, CAP)
            xd = jnp.zeros((E, CAP + 1, D), x.dtype).at[e_flat, slot].set(x[tok])
            h = _relu2(jnp.einsum('ecd,eid->eci', xd, w1))
            yd = jnp.einsum('eci,edi->ecd', h, w2)
            gate = w.reshape(-1)[:, None] * keep[:, None].astype(x.dtype)
            y_assign = yd[e_flat, slot] * gate
            return jnp.zeros((T, D), x.dtype).at[tok].add(y_assign)
        orig = hidden_states.shape
        x = hidden_states.reshape(-1, orig[-1])
        idx, wts = _router(x, gate_w, e_bias)
        shared = _relu2(x @ shared_up_w.T) @ shared_down_w.T
        routed = _moe(x, idx, wts.astype(x.dtype), w1, w2)
        return (shared + routed).reshape(orig)
    x = L0_attn_x
    x = x + _layernorm(_L0_attn_ref(_layernorm(x, axis=-1), L0_attn_w_norm, L0_attn_W_in, L0_attn_w_conv, L0_attn_dt_bias, L0_attn_A_log, L0_attn_W_h2i, L0_attn_W_out), axis=-1)
    x = x + _layernorm(_L0_ffn_ref(_layernorm(x, axis=-1), L0_ffn_gate_w, L0_ffn_e_bias, L0_ffn_w1, L0_ffn_w2, L0_ffn_shared_up_w, L0_ffn_shared_down_w), axis=-1)
    return x

_drawn_inputs = setup_inputs


def setup_inputs(seed=0):
    import zlib

    import numpy as np

    out = dict(_drawn_inputs(seed))
    spreads = {'L0_attn_w_norm': (1.0, 0.6), 'L0_ffn_e_bias': (0.0, 0.1)}
    factors = {'L0_attn_W_in': 8.0,
     'L0_attn_w_conv': 8.0,
     'L0_attn_dt_bias': 8.0,
     'L0_attn_A_log': 8.0,
     'L0_attn_W_h2i': 8.0,
     'L0_attn_W_out': 8.0}
    for name, (base, spread) in spreads.items():
        noise = np.random.default_rng([zlib.crc32(name.encode()), seed]).standard_normal(out[name].shape)
        drawn = base * np.exp(spread * noise) if base else spread * noise
        out[name] = jnp.asarray(drawn.astype(out[name].dtype))
    for name, factor in factors.items():
        out[name] = (out[name] * factor).astype(out[name].dtype)
    return out
```

```python
from contextlib import ExitStack

import numpy as np
import concourse.bass as bass
from concourse import mybir

P = 128
T, D = 1024, 256
NT = T // P
KD = D // P
DI, H, N, TAPS = 512, 16, 16, 4
CI = DI // P
HN = H * N
R = HN // P
HT = T // 2
HI = NT // 2
E, CAP, TOPK, NG, TOPG = 64, 64, 6, 8, 4
GE = E // NG
EI = 128
SHW = 512
SC = SHW // P
PAIRS = E // 2
RING = 8
LN_EPS, RMS_EPS, SCALE = 1e-5, 1.1920929e-07, 2.5
BIG = 1e30
NSLOT = E * CAP
YB = 4
YG = 2 * TOPK

F32 = mybir.dt.float32
BF16 = mybir.dt.bfloat16
U32 = mybir.dt.uint32
ALU = mybir.AluOpType
ACT = mybir.ActivationFunctionType
AX_X = mybir.AxisListType.X

XI0, DT0, B0, C0, Z0 = 0, CI, CI + R, CI + 2 * R, CI + 3 * R
NPROJ = Z0 + CI

C_ID = 0
C_SEL = C_ID + P
C_TRI = C_SEL + 2 * P
C_KEY = C_TRI + P
C_LOW = C_KEY + NT
C_EB = C_LOW + NG * NG
C_PAIR = C_EB + E
C_PAR = C_PAIR + PAIRS
C_MH = C_PAR + 2
NCONST = C_MH + 4


def constants():
    c = np.zeros((P, NCONST), np.float32)
    p = np.arange(P)
    c[:, C_ID:C_ID + P] = np.eye(P)
    for q in range(2):
        col = np.arange(P)
        hit = (col[None, :] // 64 == q) & (p[:, None] // 32 == (col[None, :] % 64) // N)
        c[:, C_SEL + q * P:C_SEL + (q + 1) * P] = hit / 32.0
    c[:, C_TRI:C_TRI + P] = p[:, None] < p[None, :]
    c[:, C_KEY:C_KEY + NT] = T - (p[:, None] + P * np.arange(NT)[None, :])
    g = np.arange(NG)
    c[:, C_LOW:C_LOW + NG * NG] = (g[None, :] < g[:, None]).reshape(-1)
    c[:, C_EB:C_EB + E] = 64 * np.arange(E) + 1
    e = p % E
    c[:, C_PAIR:C_PAIR + PAIRS] = (e[:, None] // 2) == np.arange(PAIRS)[None, :]
    c[:, C_PAR:C_PAR + 2] = (e[:, None] % 2) == np.arange(2)[None, :]
    c[:, C_MH:C_MH + 4] = -0.5
    return c


def program(nc, x, consts, w_in, chan, w_h2i, w_out, gate_w, e_bias, w_exp, w_su, w_sd, out):
    xf_dram = nc.dram_tensor("xf_rows", [T, D], F32, kind="Internal").ap()
    y_dram = nc.dram_tensor("slot_rows", [NSLOT + P, D], F32, kind="Internal").ap()
    x_v = x.rearrange("b (i p) d -> p (b i) d", p=P)
    out_v = out.rearrange("b (i p) d -> p (b i) d", p=P)
    xf_v = xf_dram.rearrange("(i p) d -> p i d", p=P)
    y_pairs = y_dram.rearrange("(j p) d -> j p d", p=P)

    with ExitStack() as ctx:
        def sb(name, shape, dt=F32):
            return ctx.enter_context(nc.sbuf_tensor(name, shape, dt))

        def sem(name):
            return ctx.enter_context(nc.semaphore(name))

        cst = sb("cst", [P, NCONST])
        ident = cst[:, C_ID:C_ID + P]
        minus_half = cst[:, C_MH:C_MH + 4]
        ones_b = sb("ones_b", [P, P], BF16)
        tri_b = sb("tri_b", [P, P], BF16)
        x_sb = sb("x_sb", [P, NT, D])
        xl_sb = sb("xl_sb", [P, NT, D])
        xn_sb = sb("xn_sb", [P, NT, D])
        xT_sb = sb("xT_sb", [P, KD, T])
        xi_sb = sb("xi_sb", [P, CI, TAPS - 1 + T])
        cv_sb = sb("cv_sb", [P, CI, T])
        sz_sb = sb("sz_sb", [P, CI, T])
        b_sb = sb("b_sb", [P, R, T])
        c_sb = sb("c_sb", [P, R, T])
        sp_sb = sb("sp_sb", [P, R, T])
        dt_sb = sb("dt_sb", [P, R, T])
        da_sb = sb("da_sb", [P, R, T])
        win_sb = sb("win_sb", [P, KD, NPROJ * P])
        wh_sb = sb("wh_sb", [P, R, DI])
        wo_sb = sb("wo_sb", [P, CI, D])
        gw_sb = sb("gw_sb", [P, KD, E])
        eb_sb = sb("eb_sb", [P, E])
        su_sb = sb("su_sb", [P, KD, SHW])
        sd_sb = sb("sd_sb", [P, SC, D])
        ch_sb = sb("ch_sb", [P, CI * TAPS + KD + 2 * R])
        taps = ch_sb[:, 0:CI * TAPS].rearrange("p (c k) -> p c k", k=TAPS)
        w_norm = ch_sb[:, CI * TAPS:CI * TAPS + KD]
        dt_bias = ch_sb[:, CI * TAPS + KD:CI * TAPS + KD + R]
        a_log = ch_sb[:, CI * TAPS + KD + R:CI * TAPS + KD + 2 * R]
        neg_a = sb("neg_a", [P, R])
        ring = sb("ring", [P, RING, 2, 2 * D])
        st = sb("st", [P, NT, 6])
        mv = sb("mv", [P, NT, 2])
        var = sb("var", [P, NT])
        rstd = sb("rstd", [P, NT])
        nmr = sb("nmr", [P, NT])
        msq = sb("msq", [P, NT])
        rms = sb("rms", [P, NT])
        hs_sb = xi_sb[:, :, 0:T]
        sz_flat = sz_sb[:, :, :].rearrange("p c t -> p (c t)")
        xg = sz_flat[:, 0:2048].rearrange("p (s d) -> p s d", s=RING)
        y_sb = sz_flat[:, 2048:2048 + YB * D].rearrange("p (s d) -> p s d", s=YB)
        xgT = sz_flat[:, 3072:3584].rearrange("p (s n) -> p s n", s=2)
        hr = sz_flat[:, 3584:3840].rearrange("p (s c) -> p s c", s=2)
        hx = sz_flat[:, 3840:4096].rearrange("p (s c) -> p s c", s=2)
        sp_flat = sp_sb[:, :, :].rearrange("p r t -> p (r t)")
        dt_flat = dt_sb[:, :, :].rearrange("p r t -> p (r t)")
        da_flat = da_sb[:, :, :].rearrange("p r t -> p (r t)")
        b_flat = b_sb[:, :, :].rearrange("p r t -> p (r t)")
        yg = cv_sb[:, :, :].rearrange("p c t -> p (c t)")[:, 0:YG * D].rearrange("p (s d) -> p s d", s=YG)
        score = sp_flat[:, 0:512].rearrange("p (i e) -> p i e", e=E)
        biased = sp_flat[:, 512:1024].rearrange("p (i e) -> p i e", e=E)
        slotk = sp_flat[:, 1024:1536].rearrange("p (i e) -> p i e", e=E)
        gatek = sp_flat[:, 1536:2048].rearrange("p (i e) -> p i e", e=E)
        t4 = [dt_flat[:, 256 * n:256 * n + 256].rearrange("p (g m) -> p g m", m=4) for n in range(2)]
        t2 = [dt_flat[:, 512 + 128 * n:640 + 128 * n].rearrange("p (g m) -> p g m", m=2) for n in range(4)]
        g1 = [dt_flat[:, 1024 + 64 * n:1088 + 64 * n] for n in range(5)]
        gmask = dt_flat[:, 1408:1472]
        cmp_a = da_flat[:, 0:512]
        cmp_b = da_flat[:, 512:1024]
        picked = da_flat[:, 1024:1536].rearrange("p (i e) -> p i e", e=E)
        keyt = da_flat[:, 1536:2048].rearrange("p (i h e) -> p i h e", i=HI, h=2)
        masked = b_flat[:, 0:NT * (E + 2)].rearrange("p (i e) -> p i e", e=E + 2)
        masked2 = b_flat[:, 544:544 + NT * (E + 2)].rearrange("p (i e) -> p i e", e=E + 2)
        top8 = b_flat[:, 1100:1100 + 8 * NT].rearrange("p (i k) -> p i k", k=8)
        slot8 = b_flat[:, 1164:1164 + 8 * NT].rearrange("p (i k) -> p i k", k=8)
        ebn = b_flat[:, 1228:1228 + E]
        work = b_flat[:, 1300:1300 + HT]
        c_flat = c_sb[:, :, :].rearrange("p r t -> p (r t)")
        lists = c_flat[:, 0:CAP]
        ltab = c_flat[:, 64:192].rearrange("p (b c) -> p b c", b=2)
        tokf = c_flat[:, 192:192 + PAIRS]
        junk = c_flat[:, 256:256 + TOPK * E].rearrange("p (k e) -> p k e", e=E)
        sel_b = sb("sel_b", [P, NT, E], BF16)
        wk = sb("wk", [P, NT, 8])
        wsum = sb("wsum", [P, NT])
        norm = sb("norm", [P, NT])
        tok_u = sb("tok_u", [P, PAIRS], U32)
        slot_u = sb("slot_u", [P, NT * 8], U32)
        fst = sb("fst", [P, 2, 6])
        fmv = sb("fmv", [P, 2, 2])
        fva = sb("fva", [P, 2])
        fsd = sb("fsd", [P, 2])
        frs = sb("frs", [P, 2])
        fnm = sb("fnm", [P, 2])
        acc = sb("acc", [P, 2, D])
        lnf = sb("lnf", [P, 2, D])
        zrow = sb("zrow", [P, D])

        bank = [ctx.enter_context(nc.psum_tensor(f"bank{n}", [P, 512], F32)) for n in range(8)]

        x_loaded = [sem(f"x_loaded{h}") for h in range(2)]
        cst_loaded = sem("cst_loaded")
        win_loaded = sem("win_loaded")
        ch_loaded = sem("ch_loaded")
        wh_loaded = sem("wh_loaded")
        wo_loaded = sem("wo_loaded")
        gw_loaded = sem("gw_loaded")
        eb_loaded = sem("eb_loaded")
        su_loaded = sem("su_loaded")
        sd_loaded = sem("sd_loaded")
        ring_loaded = [sem(f"ring_loaded{s}") for s in range(RING)]
        dve_link = sem("dve_link")
        act_link = sem("act_link")
        pads_zeroed = sem("pads_zeroed")
        var_ready = sem("var_ready")
        pow_done = sem("pow_done")
        nmr_ready = sem("nmr_ready")
        ln_ready = sem("ln_ready")
        xn_ready = sem("xn_ready")
        xT_in_psum = sem("xT_in_psum")
        xT_ready = sem("xT_ready")
        proj_done = sem("proj_done")
        dt_read = sem("dt_read")
        xi_ready = sem("xi_ready")
        conv_ready = sem("conv_ready")
        xs_ready = sem("xs_ready")
        abs_ready = sem("abs_ready")
        sp_ready = sem("sp_ready")
        dt_ready = sem("dt_ready")
        da_ready = sem("da_ready")
        b_ready = sem("b_ready")
        c_ready = sem("c_ready")
        z_ready = sem("z_ready")
        mean_done = sem("mean_done")
        mean_read = sem("mean_read")
        hc_ready = sem("hc_ready")
        h2i_done = sem("h2i_done")
        gated_ready = sem("gated_ready")
        mix_done = sem("mix_done")
        mix_read = sem("mix_read")
        xf_ready = sem("xf_ready")
        xf_stored = sem("xf_stored")
        xfT_in_psum = sem("xfT_in_psum")
        xfT_ready = sem("xfT_ready")
        logits_done = sem("logits_done")
        score_ready = sem("score_ready")
        consts_b = sem("consts_b")
        sel_ready = sem("sel_ready")
        pos_done = sem("pos_done")
        keyt_ready = sem("keyt_ready")
        keys_in_psum = sem("keys_in_psum")
        ltab_ready = sem("ltab_ready")
        tokens_done = sem("tokens_done")
        tok_ready = sem("tok_ready")
        slot_ready = sem("slot_ready")
        up_s_done = sem("up_s_done")
        up_s_read = sem("up_s_read")
        hs_ready = sem("hs_ready")
        down_s_done = sem("down_s_done")
        shared_ready = sem("shared_ready")
        gathered = [sem(f"gathered{s}") for s in range(RING)]
        gT_done = sem("gT_done")
        gT_ready = sem("gT_ready")
        up_done = sem("up_done")
        relu_ready = sem("relu_ready")
        hid_ready = sem("hid_ready")
        down_done = sem("down_done")
        y_ready = sem("y_ready")
        y_stored = [sem(f"y_stored{s}") for s in range(YB)]
        zrow_ready = sem("zrow_ready")
        zrow_stored = sem("zrow_stored")
        yg_loaded = [sem(f"yg_loaded{s}") for s in range(YG)]
        row_added = sem("row_added")
        wk_done = sem("wk_done")
        fin_link = sem("fin_link")
        lnf_ready = sem("lnf_ready")
        fvar_ready = sem("fvar_ready")
        fsd_ready = sem("fsd_ready")
        fnm_ready = sem("fnm_ready")
        fin_ready = sem("fin_ready")
        out_stored = sem("out_stored")

        block = ctx.enter_context(nc.Block())

        def load_slot(sp, s, j):
            sp.dma_start(ring[:, s, :, :].rearrange("p b n -> p (b n)"), w_exp[j, :, :]).then_inc(ring_loaded[s], 16)

        @block.sync
        def _(sp):
            sp.dma_start(x_sb[:, 0:HI, :], x_v[:, 0:HI, :]).then_inc(x_loaded[0], 16)
            sp.dma_start(cst[:], consts).then_inc(cst_loaded, 16)
            sp.dma_start(x_sb[:, HI:NT, :], x_v[:, HI:NT, :]).then_inc(x_loaded[1], 16)
            sp.dma_start(ch_sb[:], chan).then_inc(ch_loaded, 16)
            sp.dma_start(win_sb[:], w_in.rearrange("(k p) n -> p k n", p=P)).then_inc(win_loaded, 16)
            sp.dma_start(wh_sb[:], w_h2i.rearrange("(r p) n -> p r n", p=P)).then_inc(wh_loaded, 16)
            sp.dma_start(wo_sb[:], w_out.rearrange("(c p) n -> p c n", p=P)).then_inc(wo_loaded, 16)
            sp.dma_start(gw_sb[:], gate_w.rearrange("(k p) n -> p k n", p=P)).then_inc(gw_loaded, 16)
            sp.dma_start(eb_sb[:], e_bias).then_inc(eb_loaded, 16)
            sp.dma_start(su_sb[:], w_su.rearrange("(k p) n -> p k n", p=P)).then_inc(su_loaded, 16)
            sp.dma_start(sd_sb[:], w_sd.rearrange("(c p) n -> p c n", p=P)).then_inc(sd_loaded, 16)
            for s in range(RING):
                load_slot(sp, s, s)
            sp.wait_ge(zrow_ready, 1)
            sp.dma_start(y_pairs[NSLOT // P, :, :], zrow[:]).then_inc(zrow_stored, 16)
            for h in range(2):
                sp.wait_ge(xf_ready, HI * (h + 1))
                sp.dma_start(xf_v[:, HI * h:HI * (h + 1), :], xn_sb[:, HI * h:HI * (h + 1), :]).then_inc(xf_stored, 16)
            with sp.Fori(0, PAIRS // RING - 1) as it:
                for q in range(RING):
                    sp.wait_ge(y_ready, it * RING + (q + 1))
                    sp.dma_start(y_pairs[bass.ds(it * RING + q, 1), :, :].rearrange("a p d -> (a p) d"),
                                 y_sb[:, q % YB, :]).then_inc(y_stored[q % YB], 16)
                    sp.dma_start(ring[:, q, :, :].rearrange("p b n -> p (b n)"),
                                 w_exp[bass.ds(it * RING + (RING + q), 1), :, :].rearrange("a p n -> (a p) n"))\
                        .then_inc(ring_loaded[q], 16)
            for q in range(RING):
                j = PAIRS - RING + q
                sp.wait_ge(y_ready, j + 1)
                sp.dma_start(y_pairs[j, :, :], y_sb[:, q % YB, :]).then_inc(y_stored[q % YB], 16)
            with sp.Fori(0, NT // 2) as it:
                for u in range(2):
                    sp.wait_ge(fin_ready, it * 2 + (u + 1))
                    sp.dma_start(out_v[:, bass.ds(it * 2 + u, 1), :], x_sb[:, bass.ds(it * 2 + u, 1), :])\
                        .then_inc(out_stored, 16)
            sp.wait_ge(out_stored, 16 * NT)

        @block.gpsimd
        def _(pool):
            g = nc.gpsimd
            g.memset(xi_sb[:, :, 0:TAPS - 1], 0.0).then_inc(pads_zeroed, 1)
            g.memset(ones_b[:], 1.0).then_inc(consts_b, 1)
            g.memset(zrow[:], 0.0).then_inc(zrow_ready, 1)
            pool.wait_ge(cst_loaded, 16)
            g.tensor_copy(tri_b[:], cst[:, C_TRI:C_TRI + P]).then_inc(consts_b, 1)
            steps = [(var, rstd, h) for h in range(2)] + [(msq, rms, h) for h in range(2)]
            for h in range(2):
                steps += [(var, rstd, h), (var, rstd, h)]
            for n, (src, dst, h) in enumerate(steps):
                pool.wait_ge(var_ready, n + 1)
                g.tensor_tensor(out=dst[:, HI * h:HI * (h + 1)], in0=src[:, HI * h:HI * (h + 1)],
                                in1=minus_half, op=ALU.pow).then_inc(pow_done, 1)
            pool.wait_ge(tok_ready, 1)
            pool.wait_ge(xf_stored, 32)
            for j in range(PAIRS):
                if j >= RING:
                    pool.wait_ge(gT_done, j - RING + 1)
                pool.indirect_dma_start(out=xg[:, j % RING, :], out_offset=None, in_=xf_dram,
                                        in_offset=bass.IndirectOffsetOnAxis(ap=tok_u[:, j:j + 1], axis=0))\
                    .then_inc(gathered[j % RING], 16)
            pool.wait_ge(slot_ready, 1)
            for s in range(YB):
                pool.wait_ge(y_stored[s], 16 * (PAIRS // YB))
            pool.wait_ge(zrow_stored, 16)
            for n in range(NT * TOPK):
                if n >= YG:
                    pool.wait_ge(row_added, n - YG + 1)
                col = 8 * (n // TOPK) + n % TOPK
                pool.indirect_dma_start(out=yg[:, n % YG, :], out_offset=None, in_=y_dram,
                                        in_offset=bass.IndirectOffsetOnAxis(ap=slot_u[:, col:col + 1], axis=0))\
                    .then_inc(yg_loaded[n % YG], 16)

        @block.scalar
        def _(act):
            a = nc.scalar
            links = [0]

            def link(ins):
                links[0] += 1
                ins.then_inc(act_link, 1)
                act.wait_ge(act_link, links[0])

            act.wait_ge(ch_loaded, 16)
            link(a.activation(neg_a[:], a_log, ACT.Exp))
            link(a.mul(neg_a[:], neg_a[:], -1.0))

            def normalise(dst, src, i):
                a.activation(dst[:, i, :], src[:, i, :], ACT.Identity, bias=nmr[:, i:i + 1],
                             scale=rstd[:, i:i + 1]).then_inc(ln_ready, 1)

            for h in range(2):
                act.wait_ge(nmr_ready, h + 1)
                for i in range(HI * h, HI * (h + 1)):
                    normalise(xl_sb, x_sb, i)
            for h in range(2):
                for k in range(KD):
                    act.wait_ge(xT_in_psum, KD * h + k + 1)
                    a.activation(xT_sb[:, k, HT * h:HT * (h + 1)], bank[KD * h + k][:], ACT.Copy,
                                 scale=w_norm[:, k:k + 1]).then_inc(xT_ready, 1)

            def softplus_and_decay(h):
                s = slice(HT * h, HT * (h + 1))
                for r in range(R):
                    act.wait_ge(dt_read, R * h + r + 1)
                    a.activation(sp_sb[:, r, s], bank[4 + (NPROJ * h + DT0 + r) % 4][:], ACT.Abs,
                                 bias=dt_bias[:, r:r + 1]).then_inc(abs_ready, 1)
                for r in range(R):
                    act.wait_ge(abs_ready, R * h + r + 1)
                    link(a.activation(sp_sb[:, r, s], sp_sb[:, r, s], ACT.Exp, scale=-1.0))
                for r in range(R):
                    a.activation(sp_sb[:, r, s], sp_sb[:, r, s], ACT.Ln, bias=1.0).then_inc(sp_ready, 1)

            def decay(h):
                s = slice(HT * h, HT * (h + 1))
                for r in range(R):
                    act.wait_ge(dt_ready, R * h + r + 1)
                    a.activation(da_sb[:, r, s], dt_sb[:, r, s], ACT.Exp, scale=neg_a[:, r:r + 1]).then_inc(da_ready, 1)

            def leave(h, m, dst, ready, func=ACT.Copy):
                n = NPROJ * h + m
                act.wait_ge(proj_done, n + 1)
                a.activation(dst, bank[4 + n % 4][:], func).then_inc(ready, 1)

            for h in range(2):
                s = slice(HT * h, HT * (h + 1))
                for c in range(CI):
                    leave(h, XI0 + c, xi_sb[:, c, TAPS - 1 + HT * h:TAPS - 1 + HT * (h + 1)], xi_ready)
                softplus_and_decay(h)
                for r in range(R):
                    leave(h, B0 + r, b_sb[:, r, s], b_ready)
                for r in range(R):
                    leave(h, C0 + r, c_sb[:, r, s], c_ready)
                decay(h)
                for c in range(CI):
                    act.wait_ge(conv_ready, CI * h + c + 1)
                    a.activation(cv_sb[:, c, s], cv_sb[:, c, s], ACT.Silu).then_inc(xs_ready, 1)
                for c in range(CI):
                    leave(h, Z0 + c, sz_sb[:, c, s], z_ready, ACT.Silu)
            for h in range(2):
                act.wait_ge(nmr_ready, 2 + 2 * h + 1)
                for i in range(HI * h, HI * (h + 1)):
                    normalise(xl_sb, xn_sb, i)
                act.wait_ge(nmr_ready, 2 + 2 * h + 2)
                for i in range(HI * h, HI * (h + 1)):
                    a.activation(xn_sb[:, i, :], x_sb[:, i, :], ACT.Identity, bias=nmr[:, i:i + 1],
                                 scale=rstd[:, i:i + 1]).then_inc(xf_ready, 1)
                for k in range(KD):
                    act.wait_ge(xfT_in_psum, KD * h + k + 1)
                    a.activation(xT_sb[:, k, HT * h:HT * (h + 1)], bank[4 + KD * h + k][:], ACT.Copy)\
                        .then_inc(xfT_ready, 1)
            act.wait_ge(logits_done, 1)
            a.activation(score, bank[0][:].rearrange("p (i e) -> p i e", e=E), ACT.Sigmoid).then_inc(score_ready, 1)
            for n in range(2 * SC):
                m, h = n % SC, n // SC
                act.wait_ge(up_s_done, n + 1)
                dst = hs_sb[:, m, HT * h:HT * (h + 1)]
                a.activation(dst, bank[4 + n % 2][:], ACT.Relu).then_inc(up_s_read, 1)
                act.wait_ge(up_s_read, n + 1)
                a.activation(dst, dst, ACT.Square).then_inc(hs_ready, 1)
            for i in range(NT):
                act.wait_ge(down_s_done, i + 1)
                a.activation(xl_sb[:, i, :], bank[6 + i % 2][:, 0:D], ACT.Copy).then_inc(shared_ready, 1)
            with act.Fori(0, PAIRS // RING) as it:
                for q in range(RING):
                    act.wait_ge(gT_done, it * RING + (q + 1))
                    a.activation(xgT[:, q % 2, :], bank[q % 2][:, 0:D], ACT.Copy)\
                        .then_inc(gT_ready, 1)
                    act.wait_ge(up_done, it * RING + (q + 1))
                    a.activation(hr[:, q % 2, :], bank[2 + q % 2][:, 0:P], ACT.Relu).then_inc(relu_ready, 1)
            with act.Fori(0, NT // 2) as it:
                for u in range(2):
                    act.wait_ge(fvar_ready, it * 2 + (u + 1))
                    a.activation(fsd[:, u:u + 1], fva[:, u:u + 1], ACT.Sqrt)\
                        .then_inc(fsd_ready, 1)
                    act.wait_ge(fnm_ready, it * 2 + (u + 1))
                    a.activation(lnf[:, u, :], acc[:, u, :], ACT.Identity, bias=fnm[:, u:u + 1],
                                 scale=frs[:, u:u + 1]).then_inc(lnf_ready, 1)

        @block.vector
        def _(dve):
            v = nc.vector
            links = [0]

            def link(ins):
                links[0] += 1
                ins.then_inc(dve_link, 1)
                dve.wait_ge(dve_link, links[0])

            powers = [0]

            def stats(buf, i):
                link(v.bn_stats(st[:, i, :], buf[:, i, :]))
                link(v.bn_aggr(mv[:, i, :], st[:, i, :]))

            def ask_rstd(h):
                s = slice(HI * h, HI * (h + 1))
                v.tensor_scalar(var[:, s], mv[:, s, 1], LN_EPS, None, ALU.add).then_inc(var_ready, 1)
                powers[0] += 1

            def shift(h):
                s = slice(HI * h, HI * (h + 1))
                v.scalar_tensor_tensor(out=nmr[:, s], in0=mv[:, s, 0], scalar=-1.0, in1=rstd[:, s],
                                       op0=ALU.mult, op1=ALU.mult).then_inc(nmr_ready, 1)

            for h in range(2):
                dve.wait_ge(x_loaded[h], 16)
                for i in range(HI * h, HI * (h + 1)):
                    stats(x_sb, i)
                ask_rstd(h)
            for h in range(2):
                dve.wait_ge(pow_done, h + 1)
                shift(h)
            for h in range(2):
                s = slice(HI * h, HI * (h + 1))
                for i in range(HI * h, HI * (h + 1)):
                    dve.wait_ge(ln_ready, i + 1)
                    link(v.scalar_tensor_tensor(out=xn_sb[:, i, :], in0=xl_sb[:, i, :], scalar=1.0 / D,
                                                in1=xl_sb[:, i, :], op0=ALU.mult, op1=ALU.mult,
                                                accum_out=msq[:, i:i + 1]))
                v.tensor_scalar(msq[:, s], msq[:, s], RMS_EPS, None, ALU.add).then_inc(var_ready, 1)
            for h in range(2):
                dve.wait_ge(pow_done, 2 + h + 1)
                for i in range(HI * h, HI * (h + 1)):
                    v.tensor_scalar(xn_sb[:, i, :], xl_sb[:, i, :], rms[:, i:i + 1], None, ALU.mult)\
                        .then_inc(xn_ready, 1)

            def convolve(h, c):
                s = slice(HT * h, HT * (h + 1))
                dve.wait_ge(xi_ready, CI * h + c + 1)
                link(v.tensor_scalar(cv_sb[:, c, s], xi_sb[:, c, HT * h:HT * h + HT], taps[:, c, 0:1], None, ALU.mult))
                for k in range(1, TAPS):
                    ins = v.scalar_tensor_tensor(out=cv_sb[:, c, s], in0=xi_sb[:, c, HT * h + k:HT * h + k + HT],
                                                 scalar=taps[:, c, k:k + 1], in1=cv_sb[:, c, s],
                                                 op0=ALU.mult, op1=ALU.add)
                    if k < TAPS - 1:
                        link(ins)
                    else:
                        ins.then_inc(conv_ready, 1)

            def step_size(h, r):
                s = slice(HT * h, HT * (h + 1))
                n = NPROJ * h + DT0 + r
                dve.wait_ge(proj_done, n + 1)
                src = bank[4 + n % 4][:]
                v.tensor_scalar(dt_sb[:, r, s], src, dt_bias[:, r:r + 1], 0.0, ALU.add, ALU.max)\
                    .then_inc(dt_read, 1)

            def scan(h, r):
                s = slice(HT * h, HT * (h + 1))
                dve.wait_ge(mean_done, R * h + r + 1)
                v.tensor_tensor(dt_sb[:, r, s], bank[R * h + r][:], dt_sb[:, r, s], ALU.mult).then_inc(mean_read, 1)
                dve.wait_ge(mean_read, R * h + r + 1)
                dve.wait_ge(b_ready, R * h + r + 1)
                link(v.tensor_tensor(b_sb[:, r, s], dt_sb[:, r, s], b_sb[:, r, s], ALU.mult))
                first = 0.0 if h == 0 else sp_sb[:, r, HT - 1:HT]
                dve.wait_ge(da_ready, R * h + r + 1)
                link(v.tensor_tensor_scan(sp_sb[:, r, s], da_sb[:, r, s], b_sb[:, r, s], first, ALU.mult, ALU.add))
                dve.wait_ge(c_ready, R * h + r + 1)
                v.tensor_tensor(c_sb[:, r, s], sp_sb[:, r, s], c_sb[:, r, s], ALU.mult).then_inc(hc_ready, 1)

            dve.wait_ge(ch_loaded, 16)
            dve.wait_ge(pads_zeroed, 1)
            for h in range(2):
                s = slice(HT * h, HT * (h + 1))
                for c in range(CI - 1):
                    convolve(h, c)
                for r in range(R):
                    step_size(h, r)
                convolve(h, CI - 1)
                for r in range(R):
                    dve.wait_ge(sp_ready, R * h + r + 1)
                    dve.wait_ge(dt_read, R * h + r + 1)
                    v.tensor_tensor(dt_sb[:, r, s], dt_sb[:, r, s], sp_sb[:, r, s], ALU.add).then_inc(dt_ready, 1)
                    dve.wait_ge(dt_ready, R * h + r + 1)
                for r in range(R):
                    dve.wait_ge(da_ready, R * h + r + 1)
                    scan(h, r)
            for h in range(2):
                s = slice(HT * h, HT * (h + 1))
                for c in range(CI):
                    dve.wait_ge(h2i_done, CI * h + c + 1)
                    dve.wait_ge(z_ready, CI * h + c + 1)
                    v.tensor_tensor(cv_sb[:, c, s], bank[4 + c][:], sz_sb[:, c, s], ALU.mult).then_inc(gated_ready, 1)
                for i in range(HI * h, HI * (h + 1)):
                    dve.wait_ge(mix_done, i + 1)
                    v.tensor_tensor(xn_sb[:, i, :], bank[i % HI][:, 0:D], xl_sb[:, i, :], ALU.add)\
                        .then_inc(mix_read, 1)
                    dve.wait_ge(mix_read, i + 1)
                    stats(xn_sb, i)
                ask_rstd(h)
                dve.wait_ge(pow_done, 4 + 2 * h + 1)
                shift(h)
                for i in range(HI * h, HI * (h + 1)):
                    dve.wait_ge(ln_ready, NT + i + 1)
                    link(v.tensor_tensor(x_sb[:, i, :], x_sb[:, i, :], xl_sb[:, i, :], ALU.add))
                    stats(x_sb, i)
                ask_rstd(h)
                dve.wait_ge(pow_done, 4 + 2 * h + 2)
                shift(h)

            def flat(ap):
                return ap.rearrange("p i e -> p (i e)")

            def over(ap, n, m):
                return ap.unsqueeze(2).to_broadcast([P, n, m])

            dve.wait_ge(eb_loaded, 16)
            dve.wait_ge(score_ready, 1)
            link(v.tensor_tensor(biased, score, eb_sb[:].unsqueeze(1).to_broadcast([P, NT, E]), ALU.add))
            grp = flat(biased).rearrange("p (g m) -> p g m", m=GE)
            v.tensor_tensor(t4[0], grp[:, :, 0:4], grp[:, :, 4:8], ALU.max)
            link(v.tensor_tensor(t4[1], grp[:, :, 0:4], grp[:, :, 4:8], ALU.min))

            def merge(first, low_first, last, low_last, hi, tmp, lo, sec):
                v.tensor_tensor(hi, first, last, ALU.max)
                v.tensor_tensor(tmp, first, last, ALU.min)
                link(v.tensor_tensor(lo, low_first, low_last, ALU.max))
                link(v.tensor_tensor(sec, tmp, lo, ALU.max))

            merge(t4[0][:, :, 0:2], t4[1][:, :, 0:2], t4[0][:, :, 2:4], t4[1][:, :, 2:4], t2[0], t2[1], t2[2], t2[3])
            merge(t2[0][:, :, 0], t2[3][:, :, 0], t2[0][:, :, 1], t2[3][:, :, 1], g1[0], g1[1], g1[2], g1[3])
            link(v.tensor_tensor(g1[4], g1[0], g1[3], ALU.add))
            gs = g1[4].rearrange("p (i g) -> p i g", g=NG)
            cmp4 = [c.rearrange("p (i g o) -> p i g o", g=NG, o=NG) for c in (cmp_a, cmp_b)]
            other = gs.unsqueeze(2).to_broadcast([P, NT, NG, NG])
            own = gs.unsqueeze(3).to_broadcast([P, NT, NG, NG])
            low = cst[:, C_LOW:C_LOW + NG * NG].unsqueeze(1).to_broadcast([P, NT, NG * NG])
            v.tensor_tensor(cmp4[0], other, own, ALU.is_gt)
            link(v.tensor_tensor(cmp4[1], other, own, ALU.is_equal))
            cb = cmp_b.rearrange("p (i x) -> p i x", i=NT)
            link(v.tensor_tensor(cb, cb, low, ALU.mult))
            link(v.tensor_tensor(cmp_a, cmp_a, cmp_b, ALU.add))
            link(v.tensor_reduce(gmask, cmp_a.rearrange("p (g o) -> p g o", o=NG), AX_X, ALU.add))
            link(v.tensor_scalar(gmask, gmask, float(TOPG), -BIG, ALU.is_ge, ALU.mult))
            v.memset(masked[:, :, E:E + 2], BIG)
            link(v.tensor_tensor(masked[:, :, 0:E].rearrange("p i (g m) -> p i g m", m=GE),
                                 biased.rearrange("p i (g m) -> p i g m", m=GE),
                                 gmask.rearrange("p (i g) -> p i g", g=NG).unsqueeze(3).to_broadcast([P, NT, NG, GE]),
                                 ALU.add))
            for i in range(NT):
                ins = v.max(top8[:, i, :], masked[:, i, :])
            link(ins)
            for i in range(NT):
                ins = v.match_replace(out=masked2[:, i, :], in_to_replace=top8[:, i, :], in_values=masked[:, i, :],
                                      imm_value=-2.0 * BIG)
            link(ins)
            v.tensor_tensor(sel_b[:], masked[:, :, 0:E], masked2[:, :, 0:E], ALU.not_equal).then_inc(sel_ready, 1)
            dve.wait_ge(sel_ready, 1)
            link(v.tensor_tensor(picked, score, sel_b[:], ALU.mult))
            link(v.tensor_reduce(wsum[:], picked, AX_X, ALU.add))
            link(v.tensor_scalar(wsum[:], wsum[:], 1e-20, None, ALU.add))
            link(v.reciprocal(norm[:], wsum[:]))
            dve.wait_ge(pos_done, 1)
            pos = bank[1][:].rearrange("p (i e) -> p i e", e=E)
            link(v.scalar_tensor_tensor(out=biased, in0=pos, scalar=float(CAP), in1=sel_b[:], op0=ALU.is_lt, op1=ALU.mult))
            keep_h = biased.rearrange("p (h i) e -> p i h e", h=2)
            key_h = cst[:, C_KEY:C_KEY + NT].rearrange("p (h i) -> p i h", h=2).unsqueeze(3).to_broadcast([P, HI, 2, E])
            v.tensor_tensor(keyt, keep_h, key_h, ALU.mult).then_inc(keyt_ready, 1)
            v.tensor_tensor(slotk[:, 0:HI, :], pos[:, 0:HI, :],
                            cst[:, C_EB:C_EB + E].unsqueeze(1).to_broadcast([P, HI, E]), ALU.add)
            link(v.scalar_tensor_tensor(out=ebn, in0=bank[2][:, 0:E], scalar=float(CAP - 1), in1=cst[:, C_EB:C_EB + E],
                                        op0=ALU.add, op1=ALU.add))
            link(v.scalar_tensor_tensor(out=slotk[:, HI:NT, :], in0=pos[:, HI:NT, :], scalar=-1.0,
                                        in1=ebn.unsqueeze(1).to_broadcast([P, HI, E]), op0=ALU.mult, op1=ALU.add))
            link(v.tensor_tensor(slotk, slotk, biased, ALU.mult))
            v.tensor_tensor(gatek, picked, biased, ALU.mult)
            dve.wait_ge(keys_in_psum, 1)
            src = bank[3][:]
            for n in range(CAP // 8):
                link(v.max(lists[:, 8 * n:8 * n + 8], src))
                if n < CAP // 8 - 1:
                    link(v.match_replace(out=work, in_to_replace=lists[:, 8 * n:8 * n + 8], in_values=src, imm_value=0.0))
                    src = work
            for b in range(2):
                par = cst[:, C_PAR + b:C_PAR + b + 1]
                v.tensor_scalar(ltab[0:E, b, :], lists[0:E, :], par[0:E], None, ALU.mult)
                ins = v.tensor_scalar(ltab[E:P, b, :], lists[E:P, ::-1], par[E:P], None, ALU.mult)
            ins.then_inc(ltab_ready, 1)
            dve.wait_ge(tokens_done, 1)
            link(v.tensor_scalar(tokf, bank[3][:, 0:PAIRS], -1.0, float(T), ALU.mult, ALU.add))
            v.tensor_scalar(tok_u[:], tokf, float(T - 1), None, ALU.min).then_inc(tok_ready, 1)
            for i in range(NT):
                ins = v.max(slot8[:, i, :], slotk[:, i, :])
            link(ins)
            s8 = flat(slot8)
            link(v.tensor_scalar(flat(top8), s8, 0.0, float(NSLOT + 1), ALU.is_equal, ALU.mult))
            v.scalar_tensor_tensor(out=slot_u[:], in0=s8, scalar=-1.0, in1=flat(top8), op0=ALU.add, op1=ALU.add)\
                .then_inc(slot_ready, 1)

            def expert_steps(it):
                for q in range(RING):
                    dve.wait_ge(relu_ready, it * RING + (q + 1))
                    v.tensor_tensor(hx[:, q % 2, :], hr[:, q % 2, :], bank[2 + q % 2][:, 0:P], ALU.mult)\
                        .then_inc(hid_ready, 1)
                    dve.wait_ge(down_done, it * RING + (q + 1))
                    if not (type(it) is int and q < YB):
                        dve.wait_ge(y_stored[q % YB], 16 * ((RING // YB) * it + q // YB))
                    v.tensor_copy(y_sb[:, q % YB, :], bank[4 + q % 2][:, 0:D]).then_inc(y_ready, 1)
                    if q % 4 == 1:
                        tile = bass.ds(it * 2 + q // 4, 1)
                        for k in range(TOPK):
                            v.scalar_tensor_tensor(
                                out=junk[:, k, :], in0=slotk[:, tile, :].rearrange("p i e -> p (i e)"),
                                scalar=slot8[:, tile, k:k + 1].rearrange("p i e -> p (i e)"),
                                in1=gatek[:, tile, :].rearrange("p i e -> p (i e)"),
                                op0=ALU.is_equal, op1=ALU.mult,
                                accum_out=wk[:, tile, k:k + 1].rearrange("p i e -> p (i e)")).then_inc(wk_done, 1)

            expert_steps(0)
            with dve.Fori(1, PAIRS // RING) as it:
                expert_steps(it)
            dve.wait_ge(wk_done, NT * TOPK)
            link(v.scalar_tensor_tensor(out=wk[:, :, 0:TOPK], in0=wk[:, :, 0:TOPK], scalar=SCALE,
                                        in1=norm[:].unsqueeze(2).to_broadcast([P, NT, TOPK]), op0=ALU.mult, op1=ALU.mult))
            dve.wait_ge(shared_ready, NT)
            with dve.Fori(0, NT // 2) as it:
                own = [0]
                OWN = 6

                def step(ins):
                    own[0] += 1
                    ins.then_inc(fin_link, 1)
                    dve.wait_ge(fin_link, it * OWN + own[0])

                for u in range(2):
                    tile = bass.ds(it * 2 + u, 1)
                    for k in range(TOPK):
                        q = u * TOPK + k
                        dve.wait_ge(yg_loaded[q], it * 16 + 16)
                        before = acc[:, u, :] if k else xl_sb[:, tile, :].rearrange("p i d -> p (i d)")
                        v.scalar_tensor_tensor(out=acc[:, u, :], in0=yg[:, q, :],
                                               scalar=wk[:, tile, k:k + 1].rearrange("p i e -> p (i e)"), in1=before,
                                               op0=ALU.mult, op1=ALU.add).then_inc(row_added, 1)
                        dve.wait_ge(row_added, it * YG + (q + 1))
                    step(v.bn_stats(fst[:, u, :], acc[:, u, :]))
                    v.memset(junk[:, u, 0:1], 0.0)
                    step(v.bn_aggr(fmv[:, u, :], fst[:, u, :]))
                    v.tensor_scalar(fva[:, u:u + 1], fmv[:, u, 1:2], LN_EPS, None, ALU.add).then_inc(fvar_ready, 1)
                    dve.wait_ge(fsd_ready, it * 2 + (u + 1))
                    step(v.reciprocal(frs[:, u:u + 1], fsd[:, u:u + 1]))
                    v.scalar_tensor_tensor(out=fnm[:, u:u + 1], in0=fmv[:, u, 0:1], scalar=-1.0, in1=frs[:, u:u + 1],
                                           op0=ALU.mult, op1=ALU.mult).then_inc(fnm_ready, 1)
                    dve.wait_ge(lnf_ready, it * 2 + (u + 1))
                    x1 = x_sb[:, tile, :].rearrange("p i d -> p (i d)")
                    v.tensor_tensor(x1, x1, lnf[:, u, :], ALU.add).then_inc(fin_ready, 1)
                assert own[0] == OWN

        @block.tensor
        def _(pe):
            t = nc.tensor
            pe.wait_ge(cst_loaded, 16)
            for h in range(2):
                pe.wait_ge(xn_ready, HI * (h + 1))
                for k in range(KD):
                    for i in range(HI):
                        ins = t.transpose(bank[KD * h + k][:, P * i:P * (i + 1)],
                                          xn_sb[:, HI * h + i, P * k:P * (k + 1)], ident)
                    ins.then_inc(xT_in_psum, 1)

            def wait_left(n):
                h, m = divmod(n, NPROJ)
                for first, count, left in ((Z0, CI, z_ready), (C0, R, c_ready), (B0, R, b_ready),
                                           (DT0, R, abs_ready), (XI0, CI, xi_ready)):
                    if m >= first:
                        pe.wait_ge(left, count * h + m - first + 1)
                        return

            def project(h, first, last):
                for m in range(first, last):
                    n = NPROJ * h + m
                    if n >= 4:
                        wait_left(n - 4)
                    for k in range(KD):
                        ins = t.matmul(bank[4 + n % 4][:], win_sb[:, k, P * m:P * (m + 1)],
                                       xT_sb[:, k, HT * h:HT * (h + 1)], start=(k == 0), stop=(k == KD - 1))
                    ins.then_inc(proj_done, 1)

            def means(h):
                for r in range(R):
                    for q in range(2):
                        c = 2 * r + q
                        pe.wait_ge(xs_ready, CI * h + c + 1)
                        ins = t.matmul(bank[R * h + r][:], cst[:, C_SEL + P * q:C_SEL + P * (q + 1)],
                                       cv_sb[:, c, HT * h:HT * (h + 1)], start=(q == 0), stop=(q == 1))
                    ins.then_inc(mean_done, 1)

            pe.wait_ge(win_loaded, 16)
            pe.wait_ge(xT_ready, KD)
            project(0, 0, NPROJ)
            pe.wait_ge(xT_ready, 2 * KD)
            project(1, 0, B0)
            means(0)
            project(1, B0, NPROJ)
            means(1)
            pe.wait_ge(wh_loaded, 16)
            pe.wait_ge(wo_loaded, 16)
            for n in range(2 * NPROJ - 4, 2 * NPROJ):
                wait_left(n)
            for h in range(2):
                pe.wait_ge(hc_ready, R * (h + 1))
                for c in range(CI):
                    if h:
                        pe.wait_ge(gated_ready, c + 1)
                    for r in range(R):
                        ins = t.matmul(bank[4 + c][:], wh_sb[:, r, P * c:P * (c + 1)],
                                       c_sb[:, r, HT * h:HT * (h + 1)], start=(r == 0), stop=(r == R - 1))
                    ins.then_inc(h2i_done, 1)
                pe.wait_ge(gated_ready, CI * (h + 1))
                for i in range(HI * h, HI * (h + 1)):
                    if h:
                        pe.wait_ge(mix_read, i - HI + 1)
                    for c in range(CI):
                        ins = t.matmul(bank[i % HI][:, 0:D], cv_sb[:, c, P * i:P * (i + 1)], wo_sb[:, c, :],
                                       start=(c == 0), stop=(c == CI - 1))
                    ins.then_inc(mix_done, 1)
            for h in range(2):
                pe.wait_ge(xf_ready, HI * (h + 1))
                for k in range(KD):
                    for i in range(HI):
                        ins = t.transpose(bank[4 + KD * h + k][:, P * i:P * (i + 1)],
                                          xn_sb[:, HI * h + i, P * k:P * (k + 1)], ident)
                    ins.then_inc(xfT_in_psum, 1)
            pe.wait_ge(gw_loaded, 16)
            pe.wait_ge(xfT_ready, 2 * KD)
            for i in range(NT):
                for k in range(KD):
                    ins = t.matmul(bank[0][:, E * i:E * (i + 1)], xT_sb[:, k, P * i:P * (i + 1)], gw_sb[:, k, :],
                                   start=(k == 0), stop=(k == KD - 1))
            ins.then_inc(logits_done, 1)
            pe.wait_ge(su_loaded, 16)
            for n in range(2 * SC):
                m, h = n % SC, n // SC
                if n >= 2:
                    pe.wait_ge(up_s_read, n - 1)
                for k in range(KD):
                    ins = t.matmul(bank[4 + n % 2][:], su_sb[:, k, P * m:P * (m + 1)],
                                   xT_sb[:, k, HT * h:HT * (h + 1)], start=(k == 0), stop=(k == KD - 1))
                ins.then_inc(up_s_done, 1)
            pe.wait_ge(consts_b, 2)
            pe.wait_ge(sel_ready, 1)
            t.matmul(bank[1][:], tri_b[:], sel_b[:].rearrange("p i e -> p (i e)"), start=True, stop=False)
            for i in range(NT - 1):
                rest = NT - 1 - i
                t.matmul(bank[1][:, E * (i + 1):E * NT].rearrange("p (i e) -> p i e", e=E), ones_b[:],
                         sel_b[:, i, :].unsqueeze(1).to_broadcast([P, rest, E]), start=False, stop=(rest == 1))
            for i in range(HI):
                ins = t.matmul(bank[2][:, 0:E], ones_b[:], sel_b[:, i, :], start=(i == 0), stop=(i == HI - 1))
            ins.then_inc(pos_done, 1)
            pe.wait_ge(keyt_ready, 1)
            for i in range(HI):
                ins = t.transpose(bank[3][:, P * i:P * (i + 1)], keyt[:, i, :, :].rearrange("p h e -> p (h e)"), ident)
            ins.then_inc(keys_in_psum, 1)

            def shared_down(first, last):
                pe.wait_ge(sd_loaded, 16)
                for i in range(first, last):
                    pe.wait_ge(hs_ready, SC * (i // HI + 1))
                    if i >= 2:
                        pe.wait_ge(shared_ready, i - 1)
                    for m in range(SC):
                        ins = t.matmul(bank[6 + i % 2][:, 0:D], hs_sb[:, m, P * i:P * (i + 1)], sd_sb[:, m, :],
                                       start=(m == 0), stop=(m == SC - 1))
                    ins.then_inc(down_s_done, 1)

            shared_down(0, HI)
            pe.wait_ge(ltab_ready, 1)
            t.matmul(bank[3][:, 0:PAIRS], ltab.rearrange("p b c -> p (b c)"), cst[:, C_PAIR:C_PAIR + PAIRS],
                     start=True, stop=True).then_inc(tokens_done, 1)
            shared_down(HI, NT)

            def expert_steps(it):
                for q in range(RING):
                    early = type(it) is int and q < 2
                    s = q % 2
                    pe.wait_ge(gathered[q], it * 16 + 16)
                    if not early:
                        pe.wait_ge(gT_ready, it * RING + (q - 1))
                    for k in range(KD):
                        ins = t.transpose(bank[s][:, P * k:P * (k + 1)], xg[:, q, P * k:P * (k + 1)], ident)
                    ins.then_inc(gT_done, 1)
                    pe.wait_ge(ring_loaded[q], it * 16 + 16)
                    pe.wait_ge(gT_ready, it * RING + (q + 1))
                    if not early:
                        pe.wait_ge(hid_ready, it * RING + (q - 1))
                    for b in range(2):
                        for k in range(KD):
                            ins = t.matmul(bank[2 + s][:, CAP * b:CAP * (b + 1)], ring[:, q, b, P * k:P * (k + 1)],
                                           xgT[:, s, P * k + CAP * b:P * k + CAP * (b + 1)],
                                           start=(k == 0), stop=(k == KD - 1))
                    ins.then_inc(up_done, 1)
                    pe.wait_ge(hid_ready, it * RING + (q + 1))
                    if not early:
                        pe.wait_ge(y_ready, it * RING + (q - 1))
                    for b in range(2):
                        ins = t.matmul(bank[4 + s][CAP * b:CAP * (b + 1), 0:D], hx[:, s, CAP * b:CAP * (b + 1)],
                                       ring[:, q, b, D:2 * D], start=True, stop=True)
                    ins.then_inc(down_done, 1)

            expert_steps(0)
            with pe.Fori(1, PAIRS // RING) as it:
                expert_steps(it)


def kernel(L0_attn_x, L0_attn_w_norm, L0_attn_W_in, L0_attn_w_conv, L0_attn_dt_bias, L0_attn_A_log, L0_attn_W_h2i,
           L0_attn_W_out, L0_ffn_gate_w, L0_ffn_e_bias, L0_ffn_w1, L0_ffn_w2, L0_ffn_shared_up_w,
           L0_ffn_shared_down_w):
    import concourse.bacc as bacc
    from concourse.bass_utils import run_bass_kernel_spmd

    W = np.asarray(L0_attn_W_in)
    o = 2 * DI + H
    rows = [W[DI:2 * DI], np.repeat(W[2 * DI:o], N, axis=0), W[o:o + HN], W[o + HN:], W[:DI]]
    w_in = np.concatenate(rows, axis=0).T

    def by_partition(a):
        return np.asarray(a).reshape(-1, P).T

    chan = np.concatenate([
        np.asarray(L0_attn_w_conv).reshape(CI, P, TAPS).transpose(1, 0, 2).reshape(P, CI * TAPS),
        by_partition(L0_attn_w_norm),
        by_partition(np.repeat(np.asarray(L0_attn_dt_bias), N)),
        by_partition(np.repeat(np.asarray(L0_attn_A_log), N))], axis=1)
    w1 = np.asarray(L0_ffn_w1).reshape(PAIRS, 2, EI, KD, P).transpose(0, 4, 1, 3, 2).reshape(PAIRS, P, 2, KD * EI)
    w2 = np.asarray(L0_ffn_w2).reshape(PAIRS, 2, D, EI).transpose(0, 3, 1, 2)
    arrays = {
        "x": np.asarray(L0_attn_x),
        "consts": constants(),
        "w_in": w_in,
        "chan": chan,
        "w_h2i": np.repeat(np.asarray(L0_attn_W_h2i).T, N, axis=0),
        "w_out": np.asarray(L0_attn_W_out).T,
        "gate_w": np.asarray(L0_ffn_gate_w).T,
        "e_bias": np.tile(np.asarray(L0_ffn_e_bias)[None, :], (P, 1)),
        "w_exp": np.concatenate([w1, w2], axis=3).reshape(PAIRS, P, 4 * D),
        "w_su": np.asarray(L0_ffn_shared_up_w).T,
        "w_sd": np.asarray(L0_ffn_shared_down_w).T,
    }
    arrays = {n: np.ascontiguousarray(a) for n, a in arrays.items()}
    nc = bacc.Bacc("TRN2", target_bir_lowering=False, num_devices=1)
    aps = [nc.dram_tensor(f"in_{n}", a.shape, mybir.dt.from_np(a.dtype), kind="ExternalInput").ap()
           for n, a in arrays.items()]
    out = nc.dram_tensor("out_x", (1, T, D), F32, kind="ExternalOutput").ap()
    program(nc, *aps, out)
    r = run_bass_kernel_spmd(nc, [{f"in_{n}": a for n, a in arrays.items()}], core_ids=[0])
    return r.results[0]["out_x"]
```

```python
from contextlib import ExitStack

import numpy as np
import concourse.bass as bass
from concourse import mybir

P = 128
T, D = 1024, 256
NT = T // P
KD = D // P
DI, H, N, TAPS = 512, 16, 16, 4
CI = DI // P
HN = H * N
R = HN // P
HT = T // 2
HI = NT // 2
GT = 2
NGR = NT // GT
E, CAP, TOPK, NG, TOPG = 64, 64, 6, 8, 4
GE = E // NG
EI = 128
SHW = 512
SC = SHW // P
PAIRS = E // 2
RING = 8
LN_EPS, RMS_EPS, SCALE = 1e-5, 1.1920929e-07, 2.5
BIG = 1e30
NSLOT = E * CAP
YB = 4
YG = 2 * TOPK

F32 = mybir.dt.float32
BF16 = mybir.dt.bfloat16
U32 = mybir.dt.uint32
ALU = mybir.AluOpType
ACT = mybir.ActivationFunctionType
AX_X = mybir.AxisListType.X

XI0, DT0, B0, C0, Z0 = 0, CI, CI + R, CI + 2 * R, CI + 3 * R
NPROJ = Z0 + CI

C_ID = 0
C_SEL = C_ID + P
C_TRI = C_SEL + 2 * P
C_KEY = C_TRI + P
C_LOW = C_KEY + NT
C_EB = C_LOW + NG * NG
C_PAIR = C_EB + E
C_PAR = C_PAIR + PAIRS
NCONST = C_PAR + 2


def constants():
    c = np.zeros((P, NCONST), np.float32)
    p = np.arange(P)
    c[:, C_ID:C_ID + P] = np.eye(P)
    for q in range(2):
        col = np.arange(P)
        hit = (col[None, :] // 64 == q) & (p[:, None] // 32 == (col[None, :] % 64) // N)
        c[:, C_SEL + q * P:C_SEL + (q + 1) * P] = hit / 32.0
    c[:, C_TRI:C_TRI + P] = p[:, None] < p[None, :]
    c[:, C_KEY:C_KEY + NT] = T - (p[:, None] + P * np.arange(NT)[None, :])
    g = np.arange(NG)
    c[:, C_LOW:C_LOW + NG * NG] = (g[None, :] < g[:, None]).reshape(-1)
    c[:, C_EB:C_EB + E] = 64 * np.arange(E) + 1
    e = p % E
    c[:, C_PAIR:C_PAIR + PAIRS] = (e[:, None] // 2) == np.arange(PAIRS)[None, :]
    c[:, C_PAR:C_PAR + 2] = (e[:, None] % 2) == np.arange(2)[None, :]
    return c


def program(nc, x, consts, w_in, chan, w_h2i, w_out, gate_w, e_bias, w_exp, w_su, w_sd, out):
    xf_dram = nc.dram_tensor("xf_rows", [T, D], F32, kind="Internal").ap()
    y_dram = nc.dram_tensor("slot_rows", [NSLOT + P, D], F32, kind="Internal").ap()
    x_v = x.rearrange("b (i p) d -> p (b i) d", p=P)
    out_v = out.rearrange("b (i p) d -> p (b i) d", p=P)
    xf_v = xf_dram.rearrange("(i p) d -> p i d", p=P)
    y_pairs = y_dram.rearrange("(j p) d -> j p d", p=P)

    with ExitStack() as ctx:
        def sb(name, shape, dt=F32):
            return ctx.enter_context(nc.sbuf_tensor(name, shape, dt))

        def sem(name):
            return ctx.enter_context(nc.semaphore(name))

        cst = sb("cst", [P, NCONST])
        ident = cst[:, C_ID:C_ID + P]
        ones_b = sb("ones_b", [P, P], BF16)
        tri_b = sb("tri_b", [P, P], BF16)
        x_sb = sb("x_sb", [P, NT, D])
        xl_sb = sb("xl_sb", [P, NT, D])
        xn_sb = sb("xn_sb", [P, NT, D])
        xT_sb = sb("xT_sb", [P, KD, T])
        xi_sb = sb("xi_sb", [P, CI, TAPS - 1 + T])
        cv_sb = sb("cv_sb", [P, CI, T])
        sz_sb = sb("sz_sb", [P, CI, T])
        b_sb = sb("b_sb", [P, R, T])
        c_sb = sb("c_sb", [P, R, T])
        sp_sb = sb("sp_sb", [P, R, T])
        dt_sb = sb("dt_sb", [P, R, T])
        da_sb = sb("da_sb", [P, R, T])
        win_sb = sb("win_sb", [P, KD, NPROJ * P])
        wh_sb = sb("wh_sb", [P, R, DI])
        wo_sb = sb("wo_sb", [P, CI, D])
        gw_sb = sb("gw_sb", [P, KD, E])
        eb_sb = sb("eb_sb", [P, E])
        su_sb = sb("su_sb", [P, KD, SHW])
        sd_sb = sb("sd_sb", [P, SC, D])
        ch_sb = sb("ch_sb", [P, CI * TAPS + KD + 2 * R])
        taps = ch_sb[:, 0:CI * TAPS].rearrange("p (c k) -> p c k", k=TAPS)
        w_norm = ch_sb[:, CI * TAPS:CI * TAPS + KD]
        dt_bias = ch_sb[:, CI * TAPS + KD:CI * TAPS + KD + R]
        a_log = ch_sb[:, CI * TAPS + KD + R:CI * TAPS + KD + 2 * R]
        neg_a = sb("neg_a", [P, R])
        ring = sb("ring", [P, RING, 2, 2 * D])
        st = sb("st", [P, NT, 6])
        mv = sb("mv", [P, NT, 2])
        var = sb("var", [P, NT])
        rstd = sb("rstd", [P, NT])
        nmr = sb("nmr", [P, NT])
        msq = sb("msq", [P, NT])
        rms = sb("rms", [P, NT])
        std = sb("std", [P, NT])
        warm = sb("warm", [P, 3])
        hs_sb = xi_sb[:, :, 0:T]
        sz_flat = sz_sb[:, :, :].rearrange("p c t -> p (c t)")
        xg = sz_flat[:, 0:2048].rearrange("p (s d) -> p s d", s=RING)
        y_sb = sz_flat[:, 2048:2048 + YB * D].rearrange("p (s d) -> p s d", s=YB)
        xgT = sz_flat[:, 3072:3584].rearrange("p (s n) -> p s n", s=2)
        hr = sz_flat[:, 3584:3840].rearrange("p (s c) -> p s c", s=2)
        hx = sz_flat[:, 3840:4096].rearrange("p (s c) -> p s c", s=2)
        sp_flat = sp_sb[:, :, :].rearrange("p r t -> p (r t)")
        dt_flat = dt_sb[:, :, :].rearrange("p r t -> p (r t)")
        da_flat = da_sb[:, :, :].rearrange("p r t -> p (r t)")
        b_flat = b_sb[:, :, :].rearrange("p r t -> p (r t)")
        yg = cv_sb[:, :, :].rearrange("p c t -> p (c t)")[:, 0:YG * D].rearrange("p (s d) -> p s d", s=YG)
        score = sp_flat[:, 0:512].rearrange("p (i e) -> p i e", e=E)
        biased = sp_flat[:, 512:1024].rearrange("p (i e) -> p i e", e=E)
        slotk = sp_flat[:, 1024:1536].rearrange("p (i e) -> p i e", e=E)
        gatek = sp_flat[:, 1536:2048].rearrange("p (i e) -> p i e", e=E)
        t4 = [dt_flat[:, 128 * n:128 * n + 128].rearrange("p (g m) -> p g m", m=4) for n in range(2)]
        t2 = [dt_flat[:, 512 + 64 * n:576 + 64 * n].rearrange("p (g m) -> p g m", m=2) for n in range(4)]
        g1 = [dt_flat[:, 1024 + 32 * n:1056 + 32 * n] for n in range(5)]
        gmask = dt_flat[:, 1408:1440]
        cmp_a = da_flat[:, 0:256]
        cmp_b = da_flat[:, 512:768]
        picked = da_flat[:, 1024:1536].rearrange("p (i e) -> p i e", e=E)
        keyt = da_flat[:, 1536:2048].rearrange("p (i h e) -> p i h e", i=HI, h=2)
        masked = b_flat[:, 0:NT * (E + 2)].rearrange("p (i e) -> p i e", e=E + 2)
        masked2 = b_flat[:, 544:544 + NT * (E + 2)].rearrange("p (i e) -> p i e", e=E + 2)
        top8 = b_flat[:, 1100:1100 + 8 * NT].rearrange("p (i k) -> p i k", k=8)
        slot8 = b_flat[:, 1164:1164 + 8 * NT].rearrange("p (i k) -> p i k", k=8)
        ebn = b_flat[:, 1228:1228 + E]
        work = b_flat[:, 1300:1300 + HT]
        c_flat = c_sb[:, :, :].rearrange("p r t -> p (r t)")
        lists = c_flat[:, 0:CAP]
        ltab = c_flat[:, 64:192].rearrange("p (b c) -> p b c", b=2)
        tokf = c_flat[:, 192:192 + PAIRS]
        junk = c_flat[:, 256:256 + TOPK * E].rearrange("p (k e) -> p k e", e=E)
        sel_b = sb("sel_b", [P, NT, E], BF16)
        wk = sb("wk", [P, NT, 8])
        wsum = sb("wsum", [P, NT])
        norm = sb("norm", [P, NT])
        tok_u = sb("tok_u", [P, PAIRS], U32)
        slot_u = sb("slot_u", [P, NT * 8], U32)
        fst = sb("fst", [P, 2, 6])
        fmv = sb("fmv", [P, 2, 2])
        fva = sb("fva", [P, 2])
        fsd = sb("fsd", [P, 2])
        frs = sb("frs", [P, 2])
        fnm = sb("fnm", [P, 2])
        acc = sb("acc", [P, 2, D])
        lnf = sb("lnf", [P, 2, D])
        zrow = sb("zrow", [P, D])

        bank = [ctx.enter_context(nc.psum_tensor(f"bank{n}", [P, 512], F32)) for n in range(8)]

        x_loaded = [sem(f"x_loaded{g}") for g in range(NGR)]
        cst_loaded = sem("cst_loaded")
        win_loaded = sem("win_loaded")
        ch_loaded = sem("ch_loaded")
        wh_loaded = sem("wh_loaded")
        wo_loaded = sem("wo_loaded")
        gw_loaded = sem("gw_loaded")
        eb_loaded = sem("eb_loaded")
        su_loaded = sem("su_loaded")
        sd_loaded = sem("sd_loaded")
        ring_loaded = [sem(f"ring_loaded{s}") for s in range(RING)]
        dve_link = sem("dve_link")
        act_link = sem("act_link")
        pads_zeroed = sem("pads_zeroed")
        var_ready = sem("var_ready")
        std_ready = sem("std_ready")
        nmr_ready = sem("nmr_ready")
        ln_ready = sem("ln_ready")
        xn_ready = sem("xn_ready")
        xT_in_psum = sem("xT_in_psum")
        xT_ready = sem("xT_ready")
        proj_done = sem("proj_done")
        dt_read = sem("dt_read")
        xi_ready = sem("xi_ready")
        conv_ready = sem("conv_ready")
        xs_ready = sem("xs_ready")
        abs_ready = sem("abs_ready")
        sp_ready = sem("sp_ready")
        dt_ready = sem("dt_ready")
        da_ready = sem("da_ready")
        b_ready = sem("b_ready")
        c_ready = sem("c_ready")
        z_ready = sem("z_ready")
        mean_done = sem("mean_done")
        mean_read = sem("mean_read")
        hc_ready = sem("hc_ready")
        h2i_done = sem("h2i_done")
        gated_ready = sem("gated_ready")
        mix_done = sem("mix_done")
        mix_read = sem("mix_read")
        xf_ready = sem("xf_ready")
        x1_ready = sem("x1_ready")
        xf_stored = sem("xf_stored")
        xfT_in_psum = sem("xfT_in_psum")
        xfT_ready = sem("xfT_ready")
        logits_done = sem("logits_done")
        score_ready = sem("score_ready")
        consts_b = sem("consts_b")
        sel_ready = sem("sel_ready")
        pos_done = sem("pos_done")
        keyt_ready = sem("keyt_ready")
        keys_in_psum = sem("keys_in_psum")
        ltab_ready = sem("ltab_ready")
        tokens_done = sem("tokens_done")
        tok_ready = sem("tok_ready")
        slot_ready = sem("slot_ready")
        up_s_done = sem("up_s_done")
        up_s_read = sem("up_s_read")
        hs_ready = sem("hs_ready")
        down_s_done = sem("down_s_done")
        shared_ready = sem("shared_ready")
        warm_zeroed = sem("warm_zeroed")
        gathered = [sem(f"gathered{s}") for s in range(RING)]
        gT_done = sem("gT_done")
        gT_ready = sem("gT_ready")
        up_done = sem("up_done")
        relu_ready = sem("relu_ready")
        hid_ready = sem("hid_ready")
        down_done = sem("down_done")
        y_ready = sem("y_ready")
        y_stored = [sem(f"y_stored{s}") for s in range(YB)]
        zrow_ready = sem("zrow_ready")
        zrow_stored = sem("zrow_stored")
        yg_loaded = [sem(f"yg_loaded{s}") for s in range(YG)]
        row_added = sem("row_added")
        wk_done = sem("wk_done")
        fin_link = sem("fin_link")
        lnf_ready = sem("lnf_ready")
        fvar_ready = sem("fvar_ready")
        fsd_ready = sem("fsd_ready")
        fnm_ready = sem("fnm_ready")
        fin_ready = sem("fin_ready")
        out_stored = sem("out_stored")

        block = ctx.enter_context(nc.Block())

        def load_slot(sp, s, j):
            sp.dma_start(ring[:, s, :, :].rearrange("p b n -> p (b n)"), w_exp[j, :, :]).then_inc(ring_loaded[s], 16)

        @block.sync
        def _(sp):
            for g in range(NGR):
                sp.dma_start(x_sb[:, GT * g:GT * (g + 1), :], x_v[:, GT * g:GT * (g + 1), :]).then_inc(x_loaded[g], 16)
                if g == 1:
                    sp.dma_start(cst[:], consts).then_inc(cst_loaded, 16)
            sp.dma_start(ch_sb[:], chan).then_inc(ch_loaded, 16)
            sp.dma_start(win_sb[:], w_in.rearrange("(k p) n -> p k n", p=P)).then_inc(win_loaded, 16)
            sp.dma_start(wh_sb[:], w_h2i.rearrange("(r p) n -> p r n", p=P)).then_inc(wh_loaded, 16)
            sp.dma_start(wo_sb[:], w_out.rearrange("(c p) n -> p c n", p=P)).then_inc(wo_loaded, 16)
            sp.dma_start(gw_sb[:], gate_w.rearrange("(k p) n -> p k n", p=P)).then_inc(gw_loaded, 16)
            sp.dma_start(eb_sb[:], e_bias).then_inc(eb_loaded, 16)
            sp.dma_start(su_sb[:], w_su.rearrange("(k p) n -> p k n", p=P)).then_inc(su_loaded, 16)
            sp.dma_start(sd_sb[:], w_sd.rearrange("(c p) n -> p c n", p=P)).then_inc(sd_loaded, 16)
            for s in range(RING):
                load_slot(sp, s, s)
            sp.wait_ge(zrow_ready, 1)
            sp.dma_start(y_pairs[NSLOT // P, :, :], zrow[:]).then_inc(zrow_stored, 16)
            for h in range(2):
                sp.wait_ge(xf_ready, HI * (h + 1))
                sp.dma_start(xf_v[:, HI * h:HI * (h + 1), :], xn_sb[:, HI * h:HI * (h + 1), :]).then_inc(xf_stored, 16)
            with sp.Fori(0, PAIRS // RING - 1) as it:
                for q in range(RING):
                    sp.wait_ge(y_ready, it * RING + (q + 1))
                    sp.dma_start(y_pairs[bass.ds(it * RING + q, 1), :, :].rearrange("a p d -> (a p) d"),
                                 y_sb[:, q % YB, :]).then_inc(y_stored[q % YB], 16)
                    sp.dma_start(ring[:, q, :, :].rearrange("p b n -> p (b n)"),
                                 w_exp[bass.ds(it * RING + (RING + q), 1), :, :].rearrange("a p n -> (a p) n"))\
                        .then_inc(ring_loaded[q], 16)
            for q in range(RING):
                j = PAIRS - RING + q
                sp.wait_ge(y_ready, j + 1)
                sp.dma_start(y_pairs[j, :, :], y_sb[:, q % YB, :]).then_inc(y_stored[q % YB], 16)
            with sp.Fori(0, NT // 2) as it:
                for u in range(2):
                    sp.wait_ge(fin_ready, it * 2 + (u + 1))
                    sp.dma_start(out_v[:, bass.ds(it * 2 + u, 1), :], x_sb[:, bass.ds(it * 2 + u, 1), :])\
                        .then_inc(out_stored, 16)
            sp.wait_ge(out_stored, 16 * NT)

        @block.gpsimd
        def _(pool):
            g = nc.gpsimd
            g.memset(xi_sb[:, :, 0:TAPS - 1], 0.0).then_inc(pads_zeroed, 1)
            g.memset(warm[:, 0:1], 0.0).then_inc(warm_zeroed, 1)
            g.memset(ones_b[:], 1.0).then_inc(consts_b, 1)
            g.memset(zrow[:], 0.0).then_inc(zrow_ready, 1)
            pool.wait_ge(cst_loaded, 16)
            g.tensor_copy(tri_b[:], cst[:, C_TRI:C_TRI + P]).then_inc(consts_b, 1)
            for g in range(NGR):
                pool.wait_ge(ln_ready, NT + GT * (g + 1))
                gs = slice(GT * g, GT * (g + 1))
                nc.gpsimd.tensor_tensor(out=x_sb[:, gs, :], in0=x_sb[:, gs, :], in1=xl_sb[:, gs, :], op=ALU.add)\
                    .then_inc(x1_ready, 1)
            pool.wait_ge(tok_ready, 1)
            pool.wait_ge(xf_stored, 32)
            for j in range(PAIRS):
                if j >= RING:
                    pool.wait_ge(gT_done, j - RING + 1)
                pool.indirect_dma_start(out=xg[:, j % RING, :], out_offset=None, in_=xf_dram,
                                        in_offset=bass.IndirectOffsetOnAxis(ap=tok_u[:, j:j + 1], axis=0))\
                    .then_inc(gathered[j % RING], 16)
            pool.wait_ge(slot_ready, 1)
            for s in range(YB):
                pool.wait_ge(y_stored[s], 16 * (PAIRS // YB))
            pool.wait_ge(zrow_stored, 16)
            for n in range(NT * TOPK):
                if n >= YG:
                    pool.wait_ge(row_added, n - YG + 1)
                col = 8 * (n // TOPK) + n % TOPK
                pool.indirect_dma_start(out=yg[:, n % YG, :], out_offset=None, in_=y_dram,
                                        in_offset=bass.IndirectOffsetOnAxis(ap=slot_u[:, col:col + 1], axis=0))\
                    .then_inc(yg_loaded[n % YG], 16)

        @block.scalar
        def _(act):
            a = nc.scalar
            links = [0]

            def link(ins):
                links[0] += 1
                ins.then_inc(act_link, 1)
                act.wait_ge(act_link, links[0])

            roots = [0]
            act.wait_ge(warm_zeroed, 1)

            def root(src, g):
                roots[0] += 1
                act.wait_ge(var_ready, roots[0])
                a.activation(std[:, GT * g:GT * (g + 1)], src[:, GT * g:GT * (g + 1)], ACT.Sqrt).then_inc(std_ready, 1)

            def normalise(dst, src, g, n, ready):
                act.wait_ge(nmr_ready, n)
                for i in range(GT * g, GT * (g + 1)):
                    a.activation(dst[:, i, :], src[:, i, :], ACT.Identity, bias=nmr[:, i:i + 1],
                                 scale=rstd[:, i:i + 1]).then_inc(ready, 1)

            root(var, 0)
            for g in range(NGR):
                normalise(xl_sb, x_sb, g, g + 1, ln_ready)
                if g + 1 < NGR:
                    root(var, g + 1)
                root(msq, g)
            act.wait_ge(ch_loaded, 16)
            for h in range(2):
                if h == 1:
                    link(a.activation(neg_a[:], a_log, ACT.Exp))
                    link(a.mul(neg_a[:], neg_a[:], -1.0))
                for k in range(KD):
                    act.wait_ge(xT_in_psum, KD * h + k + 1)
                    a.activation(xT_sb[:, k, HT * h:HT * (h + 1)], bank[KD * h + k][:], ACT.Copy,
                                 scale=w_norm[:, k:k + 1]).then_inc(xT_ready, 1)

            def softplus_and_decay(h):
                s = slice(HT * h, HT * (h + 1))
                for r in range(R):
                    act.wait_ge(dt_read, R * h + r + 1)
                    a.activation(sp_sb[:, r, s], bank[4 + (NPROJ * h + DT0 + r) % 4][:], ACT.Abs,
                                 bias=dt_bias[:, r:r + 1]).then_inc(abs_ready, 1)
                for r in range(R):
                    act.wait_ge(abs_ready, R * h + r + 1)
                    link(a.activation(sp_sb[:, r, s], sp_sb[:, r, s], ACT.Exp, scale=-1.0))
                for r in range(R):
                    a.activation(sp_sb[:, r, s], sp_sb[:, r, s], ACT.Ln, bias=1.0).then_inc(sp_ready, 1)

            def decay(h):
                s = slice(HT * h, HT * (h + 1))
                for r in range(R):
                    act.wait_ge(dt_ready, R * h + r + 1)
                    a.activation(da_sb[:, r, s], dt_sb[:, r, s], ACT.Exp, scale=neg_a[:, r:r + 1]).then_inc(da_ready, 1)

            def leave(h, m, dst, ready, func=ACT.Copy):
                n = NPROJ * h + m
                act.wait_ge(proj_done, n + 1)
                a.activation(dst, bank[4 + n % 4][:], func).then_inc(ready, 1)

            for h in range(2):
                s = slice(HT * h, HT * (h + 1))
                for c in range(CI):
                    leave(h, XI0 + c, xi_sb[:, c, TAPS - 1 + HT * h:TAPS - 1 + HT * (h + 1)], xi_ready)
                softplus_and_decay(h)
                for r in range(R):
                    leave(h, B0 + r, b_sb[:, r, s], b_ready)
                for r in range(R):
                    leave(h, C0 + r, c_sb[:, r, s], c_ready)
                decay(h)
                for c in range(CI):
                    act.wait_ge(conv_ready, CI * h + c + 1)
                    a.activation(cv_sb[:, c, s], cv_sb[:, c, s], ACT.Silu).then_inc(xs_ready, 1)
                for c in range(CI):
                    leave(h, Z0 + c, sz_sb[:, c, s], z_ready, ACT.Silu)
            for h in range(2):
                ga, gb = 2 * h, 2 * h + 1
                n = NGR + 2 * ga
                root(var, ga)
                normalise(xl_sb, xn_sb, ga, n + 1, ln_ready)
                root(var, gb)
                root(var, ga)
                normalise(xl_sb, xn_sb, gb, n + 2, ln_ready)
                normalise(xn_sb, x_sb, ga, n + 3, xf_ready)
                root(var, gb)
                normalise(xn_sb, x_sb, gb, n + 4, xf_ready)
                a.activation(warm[:, 1 + h:2 + h], warm[:, 0:1], ACT.Sigmoid)
                for k in range(KD):
                    act.wait_ge(xfT_in_psum, KD * h + k + 1)
                    a.activation(xT_sb[:, k, HT * h:HT * (h + 1)], bank[4 + k][:], ACT.Copy).then_inc(xfT_ready, 1)
                act.wait_ge(logits_done, h + 1)
                a.activation(score[:, HI * h:HI * (h + 1), :], bank[6][:, 0:HI * E].rearrange("p (i e) -> p i e", e=E),
                             ACT.Sigmoid).then_inc(score_ready, 1)
            for n in range(2 * SC):
                m, h = n % SC, n // SC
                act.wait_ge(up_s_done, n + 1)
                dst = hs_sb[:, m, HT * h:HT * (h + 1)]
                a.activation(dst, bank[4 + n % 2][:], ACT.Relu).then_inc(up_s_read, 1)
                act.wait_ge(up_s_read, n + 1)
                a.activation(dst, dst, ACT.Square).then_inc(hs_ready, 1)
            for i in range(NT):
                act.wait_ge(down_s_done, i + 1)
                a.activation(xl_sb[:, i, :], bank[6 + i % 2][:, 0:D], ACT.Copy).then_inc(shared_ready, 1)
            with act.Fori(0, PAIRS // RING) as it:
                for q in range(RING):
                    act.wait_ge(gT_done, it * RING + (q + 1))
                    a.activation(xgT[:, q % 2, :], bank[q % 2][:, 0:D], ACT.Copy)\
                        .then_inc(gT_ready, 1)
                    act.wait_ge(up_done, it * RING + (q + 1))
                    a.activation(hr[:, q % 2, :], bank[2 + q % 2][:, 0:P], ACT.Relu).then_inc(relu_ready, 1)
            with act.Fori(0, NT // 2) as it:
                for u in range(2):
                    act.wait_ge(fvar_ready, it * 2 + (u + 1))
                    a.activation(fsd[:, u:u + 1], fva[:, u:u + 1], ACT.Sqrt)\
                        .then_inc(fsd_ready, 1)
                    act.wait_ge(fnm_ready, it * 2 + (u + 1))
                    a.activation(lnf[:, u, :], acc[:, u, :], ACT.Identity, bias=fnm[:, u:u + 1],
                                 scale=frs[:, u:u + 1]).then_inc(lnf_ready, 1)

        @block.vector
        def _(dve):
            v = nc.vector
            links = [0]

            def link(ins):
                links[0] += 1
                ins.then_inc(dve_link, 1)
                dve.wait_ge(dve_link, links[0])

            def stats(buf, g):
                tiles = range(GT * g, GT * (g + 1))
                for i in tiles:
                    ins = v.bn_stats(st[:, i, :], buf[:, i, :])
                link(ins)
                for i in tiles:
                    ins = v.bn_aggr(mv[:, i, :], st[:, i, :])
                link(ins)
                s = slice(GT * g, GT * (g + 1))
                v.tensor_scalar(var[:, s], mv[:, s, 1], LN_EPS, None, ALU.add).then_inc(var_ready, 1)

            roots = [0]

            def shift(g):
                s = slice(GT * g, GT * (g + 1))
                roots[0] += 1
                dve.wait_ge(std_ready, roots[0])
                link(v.reciprocal(rstd[:, s], std[:, s]))
                v.scalar_tensor_tensor(out=nmr[:, s], in0=mv[:, s, 0], scalar=-1.0, in1=rstd[:, s],
                                       op0=ALU.mult, op1=ALU.mult).then_inc(nmr_ready, 1)

            def mean_square(g):
                s = slice(GT * g, GT * (g + 1))
                for i in range(GT * g, GT * (g + 1)):
                    dve.wait_ge(ln_ready, i + 1)
                    ins = v.scalar_tensor_tensor(out=xn_sb[:, i, :], in0=xl_sb[:, i, :], scalar=1.0 / D,
                                                 in1=xl_sb[:, i, :], op0=ALU.mult, op1=ALU.mult,
                                                 accum_out=msq[:, i:i + 1])
                link(ins)
                v.tensor_scalar(msq[:, s], msq[:, s], RMS_EPS, None, ALU.add).then_inc(var_ready, 1)

            def rms_norm(g):
                s = slice(GT * g, GT * (g + 1))
                roots[0] += 1
                dve.wait_ge(std_ready, roots[0])
                link(v.reciprocal(rms[:, s], std[:, s]))
                for i in range(GT * g, GT * (g + 1)):
                    v.tensor_scalar(xn_sb[:, i, :], xl_sb[:, i, :], rms[:, i:i + 1], None, ALU.mult)\
                        .then_inc(xn_ready, 1)

            dve.wait_ge(x_loaded[0], 16)
            stats(x_sb, 0)
            for g in range(NGR):
                shift(g)
                if g:
                    rms_norm(g - 1)
                if g + 1 < NGR:
                    dve.wait_ge(x_loaded[g + 1], 16)
                    stats(x_sb, g + 1)
                mean_square(g)
            rms_norm(NGR - 1)

            def convolve(h, c):
                s = slice(HT * h, HT * (h + 1))
                dve.wait_ge(xi_ready, CI * h + c + 1)
                link(v.tensor_scalar(cv_sb[:, c, s], xi_sb[:, c, HT * h:HT * h + HT], taps[:, c, 0:1], None, ALU.mult))
                for k in range(1, TAPS):
                    ins = v.scalar_tensor_tensor(out=cv_sb[:, c, s], in0=xi_sb[:, c, HT * h + k:HT * h + k + HT],
                                                 scalar=taps[:, c, k:k + 1], in1=cv_sb[:, c, s],
                                                 op0=ALU.mult, op1=ALU.add)
                    if k < TAPS - 1:
                        link(ins)
                    else:
                        ins.then_inc(conv_ready, 1)

            def step_size(h, r):
                s = slice(HT * h, HT * (h + 1))
                n = NPROJ * h + DT0 + r
                dve.wait_ge(proj_done, n + 1)
                src = bank[4 + n % 4][:]
                v.tensor_scalar(dt_sb[:, r, s], src, dt_bias[:, r:r + 1], 0.0, ALU.add, ALU.max)\
                    .then_inc(dt_read, 1)

            def scan(h, r):
                s = slice(HT * h, HT * (h + 1))
                dve.wait_ge(mean_done, R * h + r + 1)
                v.tensor_tensor(dt_sb[:, r, s], bank[R * h + r][:], dt_sb[:, r, s], ALU.mult).then_inc(mean_read, 1)
                dve.wait_ge(mean_read, R * h + r + 1)
                dve.wait_ge(b_ready, R * h + r + 1)
                link(v.tensor_tensor(b_sb[:, r, s], dt_sb[:, r, s], b_sb[:, r, s], ALU.mult))
                first = 0.0 if h == 0 else sp_sb[:, r, HT - 1:HT]
                dve.wait_ge(da_ready, R * h + r + 1)
                link(v.tensor_tensor_scan(sp_sb[:, r, s], da_sb[:, r, s], b_sb[:, r, s], first, ALU.mult, ALU.add))
                dve.wait_ge(c_ready, R * h + r + 1)
                v.tensor_tensor(c_sb[:, r, s], sp_sb[:, r, s], c_sb[:, r, s], ALU.mult).then_inc(hc_ready, 1)

            def take_steps(h):
                s = slice(HT * h, HT * (h + 1))
                for c in range(CI - 1):
                    convolve(h, c)
                for r in range(R):
                    step_size(h, r)
                convolve(h, CI - 1)
                for r in range(R):
                    dve.wait_ge(sp_ready, R * h + r + 1)
                    dve.wait_ge(dt_read, R * h + r + 1)
                    v.tensor_tensor(dt_sb[:, r, s], dt_sb[:, r, s], sp_sb[:, r, s], ALU.add).then_inc(dt_ready, 1)

            dve.wait_ge(ch_loaded, 16)
            dve.wait_ge(pads_zeroed, 1)
            for h in range(2):
                take_steps(h)
                for r in range(R):
                    dve.wait_ge(dt_ready, R * h + r + 1)
                    dve.wait_ge(da_ready, R * h + r + 1)
                    scan(h, r)

            def gate(h):
                s = slice(HT * h, HT * (h + 1))
                for c in range(CI):
                    dve.wait_ge(h2i_done, CI * h + c + 1)
                    dve.wait_ge(z_ready, CI * h + c + 1)
                    v.tensor_tensor(cv_sb[:, c, s], bank[4 + c][:], sz_sb[:, c, s], ALU.mult).then_inc(gated_ready, 1)

            def mixed(g):
                for i in range(GT * g, GT * (g + 1)):
                    dve.wait_ge(mix_done, i + 1)
                    v.tensor_tensor(xn_sb[:, i, :], bank[i % HI][:, 0:D], xl_sb[:, i, :], ALU.add)\
                        .then_inc(mix_read, 1)
                dve.wait_ge(mix_read, GT * (g + 1))
                stats(xn_sb, g)

            def x1_stats(g):
                dve.wait_ge(x1_ready, g + 1)
                stats(x_sb, g)

            def layer_norms(h):
                ga, gb = 2 * h, 2 * h + 1
                mixed(ga)
                shift(ga)
                mixed(gb)
                x1_stats(ga)
                shift(gb)
                shift(ga)
                x1_stats(gb)
                shift(gb)

            def flat(ap):
                return ap.rearrange("p i e -> p (i e)")

            def merge(first, low_first, last, low_last, hi, tmp, lo, sec):
                v.tensor_tensor(hi, first, last, ALU.max)
                v.tensor_tensor(tmp, first, last, ALU.min)
                link(v.tensor_tensor(lo, low_first, low_last, ALU.max))
                link(v.tensor_tensor(sec, tmp, lo, ALU.max))

            def route(h):
                s = slice(HI * h, HI * (h + 1))
                dve.wait_ge(score_ready, h + 1)
                link(v.tensor_tensor(biased[:, s, :], score[:, s, :], eb_sb[:].unsqueeze(1).to_broadcast([P, HI, E]),
                                     ALU.add))
                grp = flat(biased[:, s, :]).rearrange("p (g m) -> p g m", m=GE)
                v.tensor_tensor(t4[0], grp[:, :, 0:4], grp[:, :, 4:8], ALU.max)
                link(v.tensor_tensor(t4[1], grp[:, :, 0:4], grp[:, :, 4:8], ALU.min))
                merge(t4[0][:, :, 0:2], t4[1][:, :, 0:2], t4[0][:, :, 2:4], t4[1][:, :, 2:4],
                      t2[0], t2[1], t2[2], t2[3])
                merge(t2[0][:, :, 0], t2[3][:, :, 0], t2[0][:, :, 1], t2[3][:, :, 1], g1[0], g1[1], g1[2], g1[3])
                link(v.tensor_tensor(g1[4], g1[0], g1[3], ALU.add))
                gs = g1[4].rearrange("p (i g) -> p i g", g=NG)
                cmp4 = [c.rearrange("p (i g o) -> p i g o", g=NG, o=NG) for c in (cmp_a, cmp_b)]
                other = gs.unsqueeze(2).to_broadcast([P, HI, NG, NG])
                own = gs.unsqueeze(3).to_broadcast([P, HI, NG, NG])
                low = cst[:, C_LOW:C_LOW + NG * NG].unsqueeze(1).to_broadcast([P, HI, NG * NG])
                v.tensor_tensor(cmp4[0], other, own, ALU.is_gt)
                link(v.tensor_tensor(cmp4[1], other, own, ALU.is_equal))
                cb = cmp_b.rearrange("p (i x) -> p i x", i=HI)
                link(v.tensor_tensor(cb, cb, low, ALU.mult))
                link(v.tensor_tensor(cmp_a, cmp_a, cmp_b, ALU.add))
                link(v.tensor_reduce(gmask, cmp_a.rearrange("p (g o) -> p g o", o=NG), AX_X, ALU.add))
                link(v.tensor_scalar(gmask, gmask, float(TOPG), -BIG, ALU.is_ge, ALU.mult))
                v.memset(masked[:, s, E:E + 2], BIG)
                link(v.tensor_tensor(masked[:, s, 0:E].rearrange("p i (g m) -> p i g m", m=GE),
                                     biased[:, s, :].rearrange("p i (g m) -> p i g m", m=GE),
                                     gmask.rearrange("p (i g) -> p i g", g=NG).unsqueeze(3)
                                     .to_broadcast([P, HI, NG, GE]), ALU.add))
                for i in range(HI * h, HI * (h + 1)):
                    ins = v.max(top8[:, i, :], masked[:, i, :])
                link(ins)
                for i in range(HI * h, HI * (h + 1)):
                    ins = v.match_replace(out=masked2[:, i, :], in_to_replace=top8[:, i, :], in_values=masked[:, i, :],
                                          imm_value=-2.0 * BIG)
                link(ins)
                v.tensor_tensor(sel_b[:, s, :], masked[:, s, 0:E], masked2[:, s, 0:E], ALU.not_equal)\
                    .then_inc(sel_ready, 1)
                dve.wait_ge(sel_ready, h + 1)
                link(v.tensor_tensor(picked[:, s, :], score[:, s, :], sel_b[:, s, :], ALU.mult))
                link(v.tensor_reduce(wsum[:, s], picked[:, s, :], AX_X, ALU.add))

            gate(0)
            layer_norms(0)
            gate(1)
            dve.wait_ge(eb_loaded, 16)
            route(0)
            layer_norms(1)
            route(1)
            link(v.tensor_scalar(wsum[:], wsum[:], 1e-20, None, ALU.add))
            link(v.reciprocal(norm[:], wsum[:]))
            dve.wait_ge(pos_done, 1)
            pos = bank[1][:].rearrange("p (i e) -> p i e", e=E)
            link(v.scalar_tensor_tensor(out=biased, in0=pos, scalar=float(CAP), in1=sel_b[:], op0=ALU.is_lt, op1=ALU.mult))
            keep_h = biased.rearrange("p (h i) e -> p i h e", h=2)
            key_h = cst[:, C_KEY:C_KEY + NT].rearrange("p (h i) -> p i h", h=2).unsqueeze(3).to_broadcast([P, HI, 2, E])
            v.tensor_tensor(keyt, keep_h, key_h, ALU.mult).then_inc(keyt_ready, 1)
            v.tensor_tensor(slotk[:, 0:HI, :], pos[:, 0:HI, :],
                            cst[:, C_EB:C_EB + E].unsqueeze(1).to_broadcast([P, HI, E]), ALU.add)
            link(v.scalar_tensor_tensor(out=ebn, in0=bank[2][:, 0:E], scalar=float(CAP - 1), in1=cst[:, C_EB:C_EB + E],
                                        op0=ALU.add, op1=ALU.add))
            link(v.scalar_tensor_tensor(out=slotk[:, HI:NT, :], in0=pos[:, HI:NT, :], scalar=-1.0,
                                        in1=ebn.unsqueeze(1).to_broadcast([P, HI, E]), op0=ALU.mult, op1=ALU.add))
            link(v.tensor_tensor(slotk, slotk, biased, ALU.mult))
            v.tensor_tensor(gatek, picked, biased, ALU.mult)
            dve.wait_ge(keys_in_psum, 1)
            src = bank[3][:]
            for n in range(CAP // 8):
                link(v.max(lists[:, 8 * n:8 * n + 8], src))
                if n < CAP // 8 - 1:
                    link(v.match_replace(out=work, in_to_replace=lists[:, 8 * n:8 * n + 8], in_values=src, imm_value=0.0))
                    src = work
            for b in range(2):
                par = cst[:, C_PAR + b:C_PAR + b + 1]
                v.tensor_scalar(ltab[0:E, b, :], lists[0:E, :], par[0:E], None, ALU.mult)
                ins = v.tensor_scalar(ltab[E:P, b, :], lists[E:P, ::-1], par[E:P], None, ALU.mult)
            ins.then_inc(ltab_ready, 1)
            dve.wait_ge(tokens_done, 1)
            link(v.tensor_scalar(tokf, bank[3][:, 0:PAIRS], -1.0, float(T), ALU.mult, ALU.add))
            v.tensor_scalar(tok_u[:], tokf, float(T - 1), None, ALU.min).then_inc(tok_ready, 1)
            for i in range(NT):
                ins = v.max(slot8[:, i, :], slotk[:, i, :])
            link(ins)
            s8 = flat(slot8)
            link(v.tensor_scalar(flat(top8), s8, 0.0, float(NSLOT + 1), ALU.is_equal, ALU.mult))
            v.scalar_tensor_tensor(out=slot_u[:], in0=s8, scalar=-1.0, in1=flat(top8), op0=ALU.add, op1=ALU.add)\
                .then_inc(slot_ready, 1)

            def expert_steps(it):
                for q in range(RING):
                    dve.wait_ge(relu_ready, it * RING + (q + 1))
                    v.tensor_tensor(hx[:, q % 2, :], hr[:, q % 2, :], bank[2 + q % 2][:, 0:P], ALU.mult)\
                        .then_inc(hid_ready, 1)
                    dve.wait_ge(down_done, it * RING + (q + 1))
                    if not (type(it) is int and q < YB):
                        dve.wait_ge(y_stored[q % YB], 16 * ((RING // YB) * it + q // YB))
                    v.tensor_copy(y_sb[:, q % YB, :], bank[4 + q % 2][:, 0:D]).then_inc(y_ready, 1)
                    if q % 4 == 1:
                        tile = bass.ds(it * 2 + q // 4, 1)
                        for k in range(TOPK):
                            v.scalar_tensor_tensor(
                                out=junk[:, k, :], in0=slotk[:, tile, :].rearrange("p i e -> p (i e)"),
                                scalar=slot8[:, tile, k:k + 1].rearrange("p i e -> p (i e)"),
                                in1=gatek[:, tile, :].rearrange("p i e -> p (i e)"),
                                op0=ALU.is_equal, op1=ALU.mult,
                                accum_out=wk[:, tile, k:k + 1].rearrange("p i e -> p (i e)")).then_inc(wk_done, 1)

            expert_steps(0)
            with dve.Fori(1, PAIRS // RING) as it:
                expert_steps(it)
            dve.wait_ge(wk_done, NT * TOPK)
            link(v.scalar_tensor_tensor(out=wk[:, :, 0:TOPK], in0=wk[:, :, 0:TOPK], scalar=SCALE,
                                        in1=norm[:].unsqueeze(2).to_broadcast([P, NT, TOPK]), op0=ALU.mult, op1=ALU.mult))
            with dve.Fori(0, NT // 2) as it:
                own = [0]
                OWN = 8

                def step(ins):
                    own[0] += 1
                    ins.then_inc(fin_link, 1)
                    dve.wait_ge(fin_link, it * OWN + own[0])

                for u in range(2):
                    tile = bass.ds(it * 2 + u, 1)
                    for k in range(TOPK):
                        q = u * TOPK + k
                        dve.wait_ge(yg_loaded[q], it * 16 + 16)
                        w = wk[:, tile, k:k + 1].rearrange("p i e -> p (i e)")
                        if k == 0:
                            v.tensor_scalar(acc[:, u, :], yg[:, q, :], w, None, ALU.mult).then_inc(row_added, 1)
                        else:
                            v.scalar_tensor_tensor(out=acc[:, u, :], in0=yg[:, q, :], scalar=w, in1=acc[:, u, :],
                                                   op0=ALU.mult, op1=ALU.add).then_inc(row_added, 1)
                        dve.wait_ge(row_added, it * YG + (q + 1))
                    dve.wait_ge(shared_ready, it * 2 + (u + 1))
                    step(v.tensor_tensor(acc[:, u, :], acc[:, u, :], xl_sb[:, tile, :].rearrange("p i d -> p (i d)"),
                                         ALU.add))
                    step(v.bn_stats(fst[:, u, :], acc[:, u, :]))
                    v.memset(junk[:, u, 0:1], 0.0)
                    step(v.bn_aggr(fmv[:, u, :], fst[:, u, :]))
                    v.tensor_scalar(fva[:, u:u + 1], fmv[:, u, 1:2], LN_EPS, None, ALU.add).then_inc(fvar_ready, 1)
                    dve.wait_ge(fsd_ready, it * 2 + (u + 1))
                    step(v.reciprocal(frs[:, u:u + 1], fsd[:, u:u + 1]))
                    v.scalar_tensor_tensor(out=fnm[:, u:u + 1], in0=fmv[:, u, 0:1], scalar=-1.0, in1=frs[:, u:u + 1],
                                           op0=ALU.mult, op1=ALU.mult).then_inc(fnm_ready, 1)
                    dve.wait_ge(lnf_ready, it * 2 + (u + 1))
                    x1 = x_sb[:, tile, :].rearrange("p i d -> p (i d)")
                    v.tensor_tensor(x1, x1, lnf[:, u, :], ALU.add).then_inc(fin_ready, 1)
                assert own[0] == OWN

        @block.tensor
        def _(pe):
            t = nc.tensor
            pe.wait_ge(cst_loaded, 16)
            for h in range(2):
                pe.wait_ge(xn_ready, HI * (h + 1))
                for k in range(KD):
                    for i in range(HI):
                        ins = t.transpose(bank[KD * h + k][:, P * i:P * (i + 1)],
                                          xn_sb[:, HI * h + i, P * k:P * (k + 1)], ident)
                    ins.then_inc(xT_in_psum, 1)

            def wait_left(n):
                h, m = divmod(n, NPROJ)
                for first, count, left in ((Z0, CI, z_ready), (C0, R, c_ready), (B0, R, b_ready),
                                           (DT0, R, abs_ready), (XI0, CI, xi_ready)):
                    if m >= first:
                        pe.wait_ge(left, count * h + m - first + 1)
                        return

            def project(h, first, last):
                for m in range(first, last):
                    n = NPROJ * h + m
                    if n >= 4:
                        wait_left(n - 4)
                    for k in range(KD):
                        ins = t.matmul(bank[4 + n % 4][:], win_sb[:, k, P * m:P * (m + 1)],
                                       xT_sb[:, k, HT * h:HT * (h + 1)], start=(k == 0), stop=(k == KD - 1))
                    ins.then_inc(proj_done, 1)

            def means(h):
                for r in range(R):
                    for q in range(2):
                        c = 2 * r + q
                        pe.wait_ge(xs_ready, CI * h + c + 1)
                        ins = t.matmul(bank[R * h + r][:], cst[:, C_SEL + P * q:C_SEL + P * (q + 1)],
                                       cv_sb[:, c, HT * h:HT * (h + 1)], start=(q == 0), stop=(q == 1))
                    ins.then_inc(mean_done, 1)

            pe.wait_ge(win_loaded, 16)
            pe.wait_ge(xT_ready, KD)
            project(0, 0, NPROJ)
            means(0)
            pe.wait_ge(xT_ready, 2 * KD)
            project(1, 0, NPROJ)
            means(1)
            pe.wait_ge(wh_loaded, 16)
            pe.wait_ge(wo_loaded, 16)
            for n in range(2 * NPROJ - 4, 2 * NPROJ):
                wait_left(n)
            def transpose_and_score(h):
                for g in range(2 * h, 2 * h + 2):
                    pe.wait_ge(xf_ready, GT * (g + 1))
                    for k in range(KD):
                        for i in range(GT * g, GT * (g + 1)):
                            ins = t.transpose(bank[4 + k][:, P * (i % HI):P * (i % HI + 1)],
                                              xn_sb[:, i, P * k:P * (k + 1)], ident)
                        if g % 2:
                            ins.then_inc(xfT_in_psum, 1)
                pe.wait_ge(xfT_ready, KD * (h + 1))
                if h:
                    pe.wait_ge(score_ready, h)
                for i in range(HI * h, HI * (h + 1)):
                    for k in range(KD):
                        ins = t.matmul(bank[6][:, E * (i % HI):E * (i % HI + 1)], xT_sb[:, k, P * i:P * (i + 1)],
                                       gw_sb[:, k, :], start=(k == 0), stop=(k == KD - 1))
                ins.then_inc(logits_done, 1)

            pe.wait_ge(gw_loaded, 16)
            for h in range(2):
                pe.wait_ge(hc_ready, R * (h + 1))
                for c in range(CI):
                    if h:
                        pe.wait_ge(gated_ready, c + 1)
                    for r in range(R):
                        ins = t.matmul(bank[4 + c][:], wh_sb[:, r, P * c:P * (c + 1)],
                                       c_sb[:, r, HT * h:HT * (h + 1)], start=(r == 0), stop=(r == R - 1))
                    ins.then_inc(h2i_done, 1)
                pe.wait_ge(gated_ready, CI * (h + 1))
                if h:
                    transpose_and_score(0)
                for i in range(HI * h, HI * (h + 1)):
                    if h:
                        pe.wait_ge(mix_read, i - HI + 1)
                    for c in range(CI):
                        ins = t.matmul(bank[i % HI][:, 0:D], cv_sb[:, c, P * i:P * (i + 1)], wo_sb[:, c, :],
                                       start=(c == 0), stop=(c == CI - 1))
                    ins.then_inc(mix_done, 1)
            transpose_and_score(1)
            pe.wait_ge(su_loaded, 16)
            for n in range(2 * SC):
                m, h = n % SC, n // SC
                if n >= 2:
                    pe.wait_ge(up_s_read, n - 1)
                for k in range(KD):
                    ins = t.matmul(bank[4 + n % 2][:], su_sb[:, k, P * m:P * (m + 1)],
                                   xT_sb[:, k, HT * h:HT * (h + 1)], start=(k == 0), stop=(k == KD - 1))
                ins.then_inc(up_s_done, 1)
            pe.wait_ge(consts_b, 2)
            pe.wait_ge(sel_ready, 2)
            t.matmul(bank[1][:], tri_b[:], sel_b[:].rearrange("p i e -> p (i e)"), start=True, stop=False)
            for i in range(NT - 1):
                rest = NT - 1 - i
                t.matmul(bank[1][:, E * (i + 1):E * NT].rearrange("p (i e) -> p i e", e=E), ones_b[:],
                         sel_b[:, i, :].unsqueeze(1).to_broadcast([P, rest, E]), start=False, stop=(rest == 1))
            for i in range(HI):
                ins = t.matmul(bank[2][:, 0:E], ones_b[:], sel_b[:, i, :], start=(i == 0), stop=(i == HI - 1))
            ins.then_inc(pos_done, 1)
            pe.wait_ge(keyt_ready, 1)
            for i in range(HI):
                ins = t.transpose(bank[3][:, P * i:P * (i + 1)], keyt[:, i, :, :].rearrange("p h e -> p (h e)"), ident)
            ins.then_inc(keys_in_psum, 1)

            pe.wait_ge(sd_loaded, 16)
            for i in range(NT):
                if i == NT - 1:
                    pe.wait_ge(ltab_ready, 1)
                    t.matmul(bank[3][:, 0:PAIRS], ltab.rearrange("p b c -> p (b c)"), cst[:, C_PAIR:C_PAIR + PAIRS],
                             start=True, stop=True).then_inc(tokens_done, 1)
                pe.wait_ge(hs_ready, SC * (i // HI + 1))
                if i >= 2:
                    pe.wait_ge(shared_ready, i - 1)
                for m in range(SC):
                    ins = t.matmul(bank[6 + i % 2][:, 0:D], hs_sb[:, m, P * i:P * (i + 1)], sd_sb[:, m, :],
                                   start=(m == 0), stop=(m == SC - 1))
                ins.then_inc(down_s_done, 1)
            def transpose_slots(it, q):
                s = q % 2
                pe.wait_ge(gathered[q], it * 16 + 16)
                if not (type(it) is int and it * RING + q < 2):
                    pe.wait_ge(gT_ready, it * RING + (q - 1))
                for k in range(KD):
                    ins = t.transpose(bank[s][:, P * k:P * (k + 1)], xg[:, q, P * k:P * (k + 1)], ident)
                ins.then_inc(gT_done, 1)

            def up(it, q):
                s = q % 2
                pe.wait_ge(ring_loaded[q], it * 16 + 16)
                pe.wait_ge(gT_ready, it * RING + (q + 1))
                if not (type(it) is int and it * RING + q < 2):
                    pe.wait_ge(hid_ready, it * RING + (q - 1))
                for b in range(2):
                    for k in range(KD):
                        ins = t.matmul(bank[2 + s][:, CAP * b:CAP * (b + 1)], ring[:, q, b, P * k:P * (k + 1)],
                                       xgT[:, s, P * k + CAP * b:P * k + CAP * (b + 1)],
                                       start=(k == 0), stop=(k == KD - 1))
                ins.then_inc(up_done, 1)

            def down(q, j):
                s = q % 2
                pe.wait_ge(hid_ready, j + 1)
                if not (type(j) is int and j < 2):
                    pe.wait_ge(y_ready, j - 1)
                for b in range(2):
                    ins = t.matmul(bank[4 + s][CAP * b:CAP * (b + 1), 0:D], hx[:, s, CAP * b:CAP * (b + 1)],
                                   ring[:, q, b, D:2 * D], start=True, stop=True)
                ins.then_inc(down_done, 1)

            def expert_steps(it, last=False):
                for q in range(RING):
                    if q + 1 < RING:
                        transpose_slots(it, q + 1)
                    elif not last:
                        transpose_slots(it + 1, 0)
                    up(it, q)
                    if q or type(it) is not int or it:
                        down((q - 1) % RING, it * RING + (q - 1))

            transpose_slots(0, 0)
            expert_steps(0)
            with pe.Fori(1, PAIRS // RING - 1) as it:
                expert_steps(it)
            expert_steps(PAIRS // RING - 1, last=True)
            down(RING - 1, PAIRS - 1)

def kernel(L0_attn_x, L0_attn_w_norm, L0_attn_W_in, L0_attn_w_conv, L0_attn_dt_bias, L0_attn_A_log, L0_attn_W_h2i,
           L0_attn_W_out, L0_ffn_gate_w, L0_ffn_e_bias, L0_ffn_w1, L0_ffn_w2, L0_ffn_shared_up_w,
           L0_ffn_shared_down_w):
    import concourse.bacc as bacc
    from concourse.bass_utils import run_bass_kernel_spmd

    W = np.asarray(L0_attn_W_in)
    o = 2 * DI + H
    rows = [W[DI:2 * DI], np.repeat(W[2 * DI:o], N, axis=0), W[o:o + HN], W[o + HN:], W[:DI]]
    w_in = np.concatenate(rows, axis=0).T

    def by_partition(a):
        return np.asarray(a).reshape(-1, P).T

    chan = np.concatenate([
        np.asarray(L0_attn_w_conv).reshape(CI, P, TAPS).transpose(1, 0, 2).reshape(P, CI * TAPS),
        by_partition(L0_attn_w_norm),
        by_partition(np.repeat(np.asarray(L0_attn_dt_bias), N)),
        by_partition(np.repeat(np.asarray(L0_attn_A_log), N))], axis=1)
    w1 = np.asarray(L0_ffn_w1).reshape(PAIRS, 2, EI, KD, P).transpose(0, 4, 1, 3, 2).reshape(PAIRS, P, 2, KD * EI)
    w2 = np.asarray(L0_ffn_w2).reshape(PAIRS, 2, D, EI).transpose(0, 3, 1, 2)
    arrays = {
        "x": np.asarray(L0_attn_x),
        "consts": constants(),
        "w_in": w_in,
        "chan": chan,
        "w_h2i": np.repeat(np.asarray(L0_attn_W_h2i).T, N, axis=0),
        "w_out": np.asarray(L0_attn_W_out).T,
        "gate_w": np.asarray(L0_ffn_gate_w).T,
        "e_bias": np.tile(np.asarray(L0_ffn_e_bias)[None, :], (P, 1)),
        "w_exp": np.concatenate([w1, w2], axis=3).reshape(PAIRS, P, 4 * D),
        "w_su": np.asarray(L0_ffn_shared_up_w).T,
        "w_sd": np.asarray(L0_ffn_shared_down_w).T,
    }
    arrays = {n: np.ascontiguousarray(a) for n, a in arrays.items()}
    nc = bacc.Bacc("TRN2", target_bir_lowering=False, num_devices=1)
    aps = [nc.dram_tensor(f"in_{n}", a.shape, mybir.dt.from_np(a.dtype), kind="ExternalInput").ap()
           for n, a in arrays.items()]
    out = nc.dram_tensor("out_x", (1, T, D), F32, kind="ExternalOutput").ap()
    program(nc, *aps, out)
    r = run_bass_kernel_spmd(nc, [{f"in_{n}": a for n, a in arrays.items()}], core_ids=[0])
    return r.results[0]["out_x"]
```

```python
from contextlib import ExitStack

import numpy as np
import concourse.bass as bass
from concourse import mybir

P = 128
T, D = 1024, 256
NT = T // P
KD = D // P
DI, H, N, TAPS = 512, 16, 16, 4
CI = DI // P
HN = H * N
R = HN // P
HT = T // 2
HI = NT // 2
GT = 2
NGR = NT // GT
E, CAP, TOPK, NG, TOPG = 64, 64, 6, 8, 4
GE = E // NG
EI = 128
SHW = 512
SC = SHW // P
H2I = ((0, 1, 4, 5), (4, 5, 6, 7))
PAIRS = E // 2
RING = 8
LN_EPS, RMS_EPS, SCALE = 1e-5, 1.1920929e-07, 2.5
BIG = 1e30
ROW = D + E
WARM = 19
CHUNKS = [(h, c) for h in range(2) for c in range(CI)]
POOL_CONV = [(1, CI - 1)]
HOTS = 4

F32 = mybir.dt.float32
F32R = mybir.dt.float32r
BF16 = mybir.dt.bfloat16
U32 = mybir.dt.uint32
ALU = mybir.AluOpType
ACT = mybir.ActivationFunctionType
AX_X = mybir.AxisListType.X

DT0, XI0, B0, C0, Z0 = 0, R, R + CI, 2 * R + CI, 3 * R + CI
NPROJ = Z0 + CI
WP = 2
NWP = NPROJ // WP

C_ID = 0
C_SEL = C_ID + P
C_TRI = C_SEL + P // 2
C_KEY = C_TRI + P
C_PAIR = C_KEY + NT
C_PAR = C_PAIR + PAIRS
C_SIDE = C_PAR + 2
NCONST = C_SIDE + 2


def constants():
    c = np.zeros((P, NCONST), np.float32)
    p = np.arange(P)
    c[:, C_ID:C_ID + P] = np.eye(P)
    c[:, C_SEL:C_SEL + P // 2] = (p[:, None] // (DI // H) == np.arange(P // 2)[None, :] // N) / (DI // H)
    c[:, C_TRI:C_TRI + P] = p[:, None] < p[None, :]
    c[:, C_KEY:C_KEY + NT] = T - (p[:, None] + P * np.arange(NT)[None, :])
    c[:, C_SIDE:C_SIDE + 2] = (p[:, None] // CAP) == np.arange(2)[None, :]
    e = p % E
    c[:, C_PAIR:C_PAIR + PAIRS] = (e[:, None] // 2) == np.arange(PAIRS)[None, :]
    c[:, C_PAR:C_PAR + 2] = (e[:, None] % 2) == np.arange(2)[None, :]
    return c


def program(nc, x, consts, w_in, chan, w_h2i, w_out, gate_w, e_bias, w_exp, w_su, w_sd, out):
    xf_dram = nc.dram_tensor("xf_rows", [T, ROW], F32, kind="Internal").ap()
    x_v = x.rearrange("b (i p) d -> p (b i) d", p=P)
    out_v = out.rearrange("b (i p) d -> p (b i) d", p=P)
    xf_v = xf_dram.rearrange("(i p) d -> p i d", p=P)

    with ExitStack() as ctx:
        def sb(name, shape, dt=F32):
            return ctx.enter_context(nc.sbuf_tensor(name, shape, dt))

        def sem(name):
            return ctx.enter_context(nc.semaphore(name))

        cst = sb("cst", [P, NCONST])
        ident = cst[:, C_ID:C_ID + P]
        ones_b = sb("ones_b", [P, P], BF16)
        tri_b = sb("tri_b", [P, P], BF16)
        with nc.sbuf_tensor("cv_sb", [P, CI, T], F32) as cv_sb:
            pass
        with nc.sbuf_tensor("cv_low", [P, CI, T], F32R) as cv_low:
            pass
        hot = sb("hot", [P, HOTS, T], F32R)
        x_sb = sb("x_sb", [P, NT, D])
        xl_sb = sb("xl_sb", [P, NT, D])
        xn_sb = sb("xn_sb", [P, NT, D])
        with nc.sbuf_tensor("xT_high", [P, KD, T], F32R) as xT_high:
            pass
        xT_sb = sb("xT_sb", [P, KD, T])
        xT_low = sb("xT_low", [P, KD, T], F32R)
        with nc.sbuf_tensor("cv_high", [P, CI, TAPS - 1 + T], F32R) as cv_high:
            pass
        xi_sb = sb("xi_sb", [P, CI, TAPS - 1 + T])
        sz_sb = sb("sz_sb", [P, CI, T])
        b_sb = sb("b_sb", [P, R, T])
        c_sb = sb("c_sb", [P, R, T])
        sp_sb = sb("sp_sb", [P, R, T])
        dt_sb = sb("dt_sb", [P, R, T])
        da_sb = sb("da_sb", [P, R, T])
        w_high = sb("w_high", [P, KD, NPROJ * P], F32R)
        with nc.sbuf_tensor("wh_sb", [P, R, DI], F32) as wh_sb:
            pass
        wh_low = sb("wh_low", [P, R, DI], F32R)
        with nc.sbuf_tensor("wo_sb", [P, CI, D], F32) as wo_sb:
            pass
        wo_low = sb("wo_low", [P, CI, D], F32R)
        wh_high = sb("wh_high", [P, R, DI], F32R)
        wo_high = sb("wo_high", [P, CI, D], F32R)
        gw_sb = sb("gw_sb", [P, KD, E])
        eb_sb = sb("eb_sb", [P, E])
        su_sb = sb("su_sb", [P, KD, SHW])
        sd_sb = sb("sd_sb", [P, SC, D])
        ch_sb = sb("ch_sb", [P, CI * TAPS + KD + 2 * R])
        taps = ch_sb[:, 0:CI * TAPS].rearrange("p (c k) -> p c k", k=TAPS)
        w_norm = ch_sb[:, CI * TAPS:CI * TAPS + KD]
        dt_bias = ch_sb[:, CI * TAPS + KD:CI * TAPS + KD + R]
        a_log = ch_sb[:, CI * TAPS + KD + R:CI * TAPS + KD + 2 * R]
        neg_a = sb("neg_a", [P, R])
        with nc.sbuf_tensor("w_full", [P, KD, NPROJ * P], F32) as w_full:
            with nc.sbuf_tensor("w_low", [P, KD, NPROJ * P], F32R) as w_low:
                pass
        ring = sb("ring", [P, RING, 2, 2 * D])
        st = sb("st", [P, NT, 6])
        mv = sb("mv", [P, NT, 2])
        var = sb("var", [P, NT])
        rstd = sb("rstd", [P, NT])
        nmr = sb("nmr", [P, NT])
        msq = sb("msq", [P, NT])
        rms = sb("rms", [P, NT])
        both = sb("both", [P, NT])
        nmb = sb("nmb", [P, NT])
        std = sb("std", [P, NT])
        hs_sb = xi_sb[:, :, 0:T]
        sz_flat = sz_sb[:, :, :].rearrange("p c t -> p (c t)")
        xg = sz_flat[:, 0:RING * ROW].rearrange("p (s d) -> p s d", s=RING)
        xgT = sz_flat[:, 2560:3072].rearrange("p (s n) -> p s n", s=2)
        hT = sz_flat[:, 3072:3328].rearrange("p (s c) -> p s c", s=2)
        hx = sz_flat[:, 3328:3584].rearrange("p (s c) -> p s c", s=2)
        hr = sz_flat[:, 3584:3840].rearrange("p (s c) -> p s c", s=2)
        sp_flat = sp_sb[:, :, :].rearrange("p r t -> p (r t)")
        dt_flat = dt_sb[:, :, :].rearrange("p r t -> p (r t)")
        da_flat = da_sb[:, :, :].rearrange("p r t -> p (r t)")
        b_flat = b_sb[:, :, :].rearrange("p r t -> p (r t)")
        token_no = c_sb[:, 1, :]
        score = sp_flat[:, 0:512].rearrange("p (i e) -> p i e", e=E)
        biased = sp_flat[:, 512:1024].rearrange("p (i e) -> p i e", e=E)
        NE, NR = HI * E, NT * NG
        t4 = [dt_flat[:, NE // 2 * n:NE // 2 * (n + 1)].rearrange("p (g m) -> p g m", m=4) for n in range(2)]
        t2 = [dt_flat[:, NE + NE // 4 * n:NE + NE // 4 * (n + 1)].rearrange("p (g m) -> p g m", m=2) for n in range(4)]
        g1 = [dt_flat[:, 2 * NE + NR // 2 * n:2 * NE + NR // 2 * (n + 1)] for n in range(4)]
        gs, gmask, gtop, gleft = [dt_flat[:, 2 * NE + NR * n:2 * NE + NR * (n + 1)].rearrange("p (i g) -> p i g", g=NG)
                                  for n in range(2, 6)]
        picked = da_flat[:, 1024:1536].rearrange("p (i e) -> p i e", e=E)
        keyt = da_flat[:, 1536:2048].rearrange("p (i h e) -> p i h e", i=HI, h=2)
        masked = b_flat[:, 0:NT * (E + 2)].rearrange("p (i e) -> p i e", e=E + 2)
        masked2 = b_flat[:, 544:544 + NT * (E + 2)].rearrange("p (i e) -> p i e", e=E + 2)
        top8 = b_flat[:, 1100:1100 + 8 * NT].rearrange("p (i k) -> p i k", k=8)
        work = b_flat[:, 1300:1300 + HT]
        c_flat = c_sb[:, :, :].rearrange("p r t -> p (r t)")
        lists = c_flat[:, 0:CAP]
        ltab = c_flat[:, 64:192].rearrange("p (b c) -> p b c", b=2)
        tokf = c_flat[:, 192:192 + PAIRS]
        sel_b = sb("sel_b", [P, NT, E], BF16)
        wsum = sb("wsum", [P, NT])
        norm = sb("norm", [P, NT])
        tok_u = sb("tok_u", [P, PAIRS], U32)
        with nc.sbuf_tensor("conv_part", [P, 2, HT], F32) as conv_part:
            pass
        y_parts = sb("y_parts", [P, 2, 2, D], F32R)
        gate_s = sb("gate_s", [P, RING])
        gate2 = sb("gate2", [P, RING, 2])

        bank = [ctx.enter_context(nc.psum_tensor(f"bank{n}", [P, 512], F32)) for n in range(8)]
        total = [bank[4 + i // 2][:, D * (i % 2):D * (i % 2 + 1)] for i in range(NT)]

        def rows(buf):
            return [buf[:, i, :] for i in range(NT)]


        x_loaded = [sem(f"x_loaded{g}") for g in range(NGR)]
        cst_loaded = sem("cst_loaded")
        win_loaded = [sem(f"win_loaded{p}") for p in range(NWP)]
        w_high_ready = sem("w_high_ready")
        w_low_ready = sem("w_low_ready")
        ch_loaded = sem("ch_loaded")
        wh_loaded = sem("wh_loaded")
        wo_loaded = sem("wo_loaded")
        gw_loaded = sem("gw_loaded")
        eb_loaded = sem("eb_loaded")
        su_loaded = sem("su_loaded")
        sd_loaded = sem("sd_loaded")
        ring_loaded = [sem(f"ring_loaded{s}") for s in range(RING)]
        dve_link = sem("dve_link")
        act_link = sem("act_link")
        pads_zeroed = sem("pads_zeroed")
        var_ready = sem("var_ready")
        std_ready = sem("std_ready")
        nmr_ready = sem("nmr_ready")
        ln_ready = sem("ln_ready")
        xn_ready = sem("xn_ready")
        xT_in_psum = sem("xT_in_psum")
        xT_high_ready = sem("xT_high_ready")
        xT_low_ready = sem("xT_low_ready")
        proj_done = sem("proj_done")
        dt_read = sem("dt_read")
        xi_ready = sem("xi_ready")
        conv_ready = sem("conv_ready")
        conv_pool_ready = sem("conv_pool_ready")
        pool_link = sem("pool_link")
        mixw_high_ready = sem("mixw_high_ready")
        mixw_ready = sem("mixw_ready")
        c_high_ready = sem("c_high_ready")
        c_low_ready = sem("c_low_ready")
        cv_high_ready = sem("cv_high_ready")
        cv_low_ready = sem("cv_low_ready")
        cv_low_late = sem("cv_low_late")
        xs_ready = sem("xs_ready")
        abs_ready = sem("abs_ready")
        sp_ready = sem("sp_ready")
        dt_ready = sem("dt_ready")
        da_ready = sem("da_ready")
        b_ready = sem("b_ready")
        c_ready = sem("c_ready")
        z_ready = sem("z_ready")
        mean_done = sem("mean_done")
        mean_read = sem("mean_read")
        hc_ready = sem("hc_ready")
        h2i_done = sem("h2i_done")
        gated_ready = sem("gated_ready")
        mix_done = sem("mix_done")
        mix_read = sem("mix_read")
        xf_ready = sem("xf_ready")
        x1_ready = sem("x1_ready")
        xf_stored = sem("xf_stored")
        xfT_in_psum = sem("xfT_in_psum")
        xfT_ready = sem("xfT_ready")
        logits_done = sem("logits_done")
        score_ready = sem("score_ready")
        consts_b = sem("consts_b")
        sel_ready = sem("sel_ready")
        pos_done = sem("pos_done")
        keyt_ready = sem("keyt_ready")
        keys_in_psum = sem("keys_in_psum")
        ltab_ready = sem("ltab_ready")
        tokens_done = sem("tokens_done")
        tok_ready = sem("tok_ready")
        norm_ready = sem("norm_ready")
        gates_ready = sem("gates_ready")
        token_no_ready = sem("token_no_ready")
        up_s_done = sem("up_s_done")
        up_s_read = sem("up_s_read")
        hs_ready = sem("hs_ready")
        gathered = [sem(f"gathered{s}") for s in range(RING)]
        gT_done = sem("gT_done")
        gT_ready = sem("gT_ready")
        up_done = sem("up_done")
        relu_ready = sem("relu_ready")
        hT_done = sem("hT_done")
        hT_ready = sem("hT_ready")
        hid_ready = sem("hid_ready")
        down_done = sem("down_done")
        gate_ready = sem("gate_ready")
        hot_ready = sem("hot_ready")
        y_high_ready = sem("y_high_ready")
        y_low_ready = sem("y_low_ready")
        added = sem("added")
        sum_done = sem("sum_done")
        fin_ready = sem("fin_ready")
        fin_last = sem("fin_last")
        out_stored = sem("out_stored")

        block = ctx.enter_context(nc.Block())

        def load_slot(sp, s, j):
            sp.dma_start(ring[:, s, :, :].rearrange("p b n -> p (b n)"), w_exp[j, :, :]).then_inc(ring_loaded[s], 16)

        @block.sync
        def _(sp):
            w_v = w_in.rearrange("(k p) n -> p k n", p=P)
            for g in range(NGR):
                sp.dma_start(x_sb[:, GT * g:GT * (g + 1), :], x_v[:, GT * g:GT * (g + 1), :]).then_inc(x_loaded[g], 16)
                if g == 1:
                    sp.dma_start(cst[:], consts).then_inc(cst_loaded, 16)
                    sp.dma_start(ch_sb[:], chan).then_inc(ch_loaded, 16)
                for p in {1: (0, 1, 2), 3: range(3, NWP)}.get(g, ()):
                    cols = slice(WP * P * p, WP * P * (p + 1))
                    sp.dma_start(w_full[:, :, cols], w_v[:, :, cols]).then_inc(win_loaded[p], 16)
            sp.dma_start(wh_sb[:], w_h2i.rearrange("(r p) n -> p r n", p=P)).then_inc(wh_loaded, 16)
            sp.dma_start(wo_sb[:], w_out.rearrange("(c p) n -> p c n", p=P)).then_inc(wo_loaded, 16)
            sp.dma_start(gw_sb[:], gate_w.rearrange("(k p) n -> p k n", p=P)).then_inc(gw_loaded, 16)
            sp.dma_start(eb_sb[:], e_bias).then_inc(eb_loaded, 16)
            sp.dma_start(su_sb[:], w_su.rearrange("(k p) n -> p k n", p=P)).then_inc(su_loaded, 16)
            sp.dma_start(sd_sb[:], w_sd.rearrange("(c p) n -> p c n", p=P)).then_inc(sd_loaded, 16)
            sp.wait_ge(proj_done, 2 * NPROJ)
            for s in range(RING):
                load_slot(sp, s, s)
            for h in range(2):
                sp.wait_ge(xf_ready, HI * (h + 1))
                sp.dma_start(xf_v[:, HI * h:HI * (h + 1), 0:D], xn_sb[:, HI * h:HI * (h + 1), :]).then_inc(xf_stored, 16)
            sp.wait_ge(gates_ready, 1)
            sp.dma_start(xf_v[:, :, D:ROW], picked).then_inc(xf_stored, 16)
            with sp.Fori(0, PAIRS // RING - 1) as it:
                for q in range(RING):
                    sp.wait_ge(down_done, it * RING + (q + 1))
                    sp.dma_start(ring[:, q, :, :].rearrange("p b n -> p (b n)"),
                                 w_exp[bass.ds(it * RING + (RING + q), 1), :, :].rearrange("a p n -> (a p) n"))\
                        .then_inc(ring_loaded[q], 16)
            for g in range(NGR):
                if g < NGR - 1:
                    sp.wait_ge(fin_ready, g + 1)
                else:
                    sp.wait_ge(fin_last, GT)
                sp.dma_start(out_v[:, GT * g:GT * (g + 1), :], x_sb[:, GT * g:GT * (g + 1), :]).then_inc(out_stored, 16)
            sp.wait_ge(out_stored, 16 * NGR)

        @block.gpsimd
        def _(pool):
            g = nc.gpsimd
            g.memset(xi_sb[:, :, 0:TAPS - 1], 0.0).then_inc(pads_zeroed, 1)
            g.memset(ones_b[:], 1.0).then_inc(consts_b, 1)
            pool.wait_ge(cst_loaded, 16)
            g.tensor_copy(tri_b[:], cst[:, C_TRI:C_TRI + P]).then_inc(consts_b, 1)
            for p in range(NWP):
                cols = slice(WP * P * p, WP * P * (p + 1))
                pool.wait_ge(win_loaded[p], 16)
                pool.wait_ge(w_high_ready, p + 1)
                g.tensor_tensor(out=w_low[:, :, cols], in0=w_full[:, :, cols], in1=w_high[:, :, cols].bitcast(F32),
                                op=ALU.subtract).then_inc(w_low_ready, 1)
            for i in range(NT):
                pool.wait_ge(nmr_ready, i // HI + 1)
                g.tensor_scalar(xl_sb[:, i, :], x_sb[:, i, :], rstd[:, i:i + 1], nmr[:, i:i + 1], ALU.mult, ALU.add)\
                    .then_inc(ln_ready, 1)
            for n, (full, high, low, loaded) in enumerate(((wh_sb, wh_high, wh_low, wh_loaded),
                                                           (wo_sb, wo_high, wo_low, wo_loaded))):
                pool.wait_ge(loaded, 16)
                g.tensor_copy(high[:], full[:]).then_inc(mixw_high_ready, 1)
                pool.wait_ge(mixw_high_ready, n + 1)
                g.tensor_tensor(out=low[:], in0=full[:], in1=high[:].bitcast(F32), op=ALU.subtract)\
                    .then_inc(mixw_ready, 1)
            steps = 0
            for h, c in POOL_CONV:
                pool.wait_ge(xi_ready, CI * h + c + 1)
                s = slice(HT * h, HT * (h + 1))

                def product(k, dst):
                    return g.tensor_scalar(dst, xi_sb[:, c, HT * h + k:HT * h + k + HT], taps[:, c, k:k + 1], None, ALU.mult)

                product(0, cv_sb[:, c, s])
                for k in range(1, TAPS):
                    product(k, conv_part[:, k % 2, :]).then_inc(pool_link, 1)
                    steps += 1
                    pool.wait_ge(pool_link, steps)
                    g.tensor_tensor(out=cv_sb[:, c, s], in0=cv_sb[:, c, s], in1=conv_part[:, k % 2, :], op=ALU.add)\
                        .then_inc(pool_link if k < TAPS - 1 else conv_pool_ready, 1)
                    steps += k < TAPS - 1
            def mixed_low(h, first, last):
                s = slice(HT * h, HT * (h + 1))
                for c in range(first, last):
                    pool.wait_ge(cv_high_ready, CI * h + c + 1)
                    nc.gpsimd.tensor_tensor(out=cv_low[:, c, s], in0=cv_sb[:, c, s],
                                            in1=cv_high[:, c, s].bitcast(F32), op=ALU.subtract).then_inc(cv_low_ready, 1)

            mixed_low(0, 0, CI)
            mixed_low(1, 0, 2)
            for g in range(NGR):
                pool.wait_ge(ln_ready, NT + GT * (g + 1))
                gs = slice(GT * g, GT * (g + 1))
                nc.gpsimd.tensor_tensor(out=x_sb[:, gs, :], in0=x_sb[:, gs, :], in1=xl_sb[:, gs, :], op=ALU.add)\
                    .then_inc(x1_ready, 1)
            pool.wait_ge(h2i_done, 2 * CI)
            nc.gpsimd.iota(token_no, pattern=[[1, T]], base=0, channel_multiplier=0,
                           allow_small_or_imprecise_dtypes=True).then_inc(token_no_ready, 1)
            pool.wait_ge(norm_ready, 1)
            nc.gpsimd.tensor_tensor(out=picked, in0=picked, in1=norm[:].unsqueeze(2).to_broadcast([P, NT, E]),
                                    op=ALU.mult).then_inc(gates_ready, 1)
            pool.wait_ge(tok_ready, 1)
            pool.wait_ge(xf_stored, 48)
            for j in range(PAIRS):
                if j >= RING:
                    pool.wait_ge(gT_done, j - RING + 1)
                    pool.wait_ge(gate_ready, j - RING + 1)
                pool.indirect_dma_start(out=xg[:, j % RING, :], out_offset=None, in_=xf_dram,
                                        in_offset=bass.IndirectOffsetOnAxis(ap=tok_u[:, j:j + 1], axis=0))\
                    .then_inc(gathered[j % RING], 16)
            for g in range(NGR - 1):
                pool.wait_ge(ln_ready, 2 * NT + GT * (g + 1))
                gs = slice(GT * g, GT * (g + 1))
                nc.gpsimd.tensor_tensor(out=x_sb[:, gs, :], in0=x_sb[:, gs, :], in1=xl_sb[:, gs, :], op=ALU.add)\
                    .then_inc(fin_ready, 1)

        @block.scalar
        def _(act):
            a = nc.scalar
            links = [0]

            def link(ins):
                links[0] += 1
                ins.then_inc(act_link, 1)
                act.wait_ge(act_link, links[0])

            roots = [0]
            a.preload_act_table(ACT.Sqrt)

            def root(src, s):
                roots[0] += 1
                act.wait_ge(var_ready, roots[0])
                a.activation(std[:, s], src[:, s], ACT.Sqrt).then_inc(std_ready, 1)

            def group(g):
                return slice(GT * g, GT * (g + 1))

            def half(h):
                return slice(HI * h, HI * (h + 1))

            def normalise(dst, src, g, n, ready):
                act.wait_ge(nmr_ready, n)
                for i in range(GT * g, GT * (g + 1)):
                    a.activation(dst[:, i, :], src[i], ACT.Identity, bias=nmr[:, i:i + 1],
                                 scale=rstd[:, i:i + 1]).then_inc(ready, 1)

            def x_high(h):
                for k in range(KD):
                    act.wait_ge(xT_in_psum, KD * h + k + 1)
                    a.activation(xT_high[:, k, HT * h:HT * (h + 1)], bank[KD * h + k][:], ACT.Copy,
                                 scale=w_norm[:, k:k + 1]).then_inc(xT_high_ready, 1)

            def weights_high(first, last):
                for p in range(first, last):
                    cols = slice(WP * P * p, WP * P * (p + 1))
                    act.wait_ge(win_loaded[p], 16)
                    a.activation(w_high[:, :, cols], w_full[:, :, cols], ACT.Copy).then_inc(w_high_ready, 1)

            root(var, half(0))
            weights_high(0, 1)
            root(msq, half(0))
            weights_high(1, 3)
            act.wait_ge(ch_loaded, 16)
            x_high(0)
            weights_high(3, NWP)
            root(var, half(1))
            root(msq, half(1))
            a.preload_act_table_set("natural_log_exp_and_others")
            link(a.activation(neg_a[:], a_log, ACT.Exp))
            link(a.mul(neg_a[:], neg_a[:], -1.0))

            def dt_abs(h):
                s = slice(HT * h, HT * (h + 1))
                for r in range(R):
                    act.wait_ge(dt_read, R * h + r + 1)
                    a.activation(sp_sb[:, r, s], bank[4 + (NPROJ * h + DT0 + r) % 4][:], ACT.Abs,
                                 bias=dt_bias[:, r:r + 1]).then_inc(abs_ready, 1)

            def log_term(h):
                s = slice(HT * h, HT * (h + 1))
                for r in range(R):
                    act.wait_ge(abs_ready, R * h + r + 1)
                    link(a.activation(sp_sb[:, r, s], sp_sb[:, r, s], ACT.Exp, scale=-1.0))
                for r in range(R):
                    a.activation(sp_sb[:, r, s], sp_sb[:, r, s], ACT.Ln, bias=1.0).then_inc(sp_ready, 1)

            def decay(h):
                s = slice(HT * h, HT * (h + 1))
                for r in range(R):
                    act.wait_ge(dt_ready, R * h + r + 1)
                    a.activation(da_sb[:, r, s], dt_sb[:, r, s], ACT.Exp, scale=neg_a[:, r:r + 1]).then_inc(da_ready, 1)

            def leave(h, m, dst, ready, func=ACT.Copy):
                n = NPROJ * h + m
                act.wait_ge(proj_done, n + 1)
                a.activation(dst, bank[4 + n % 4][:], func).then_inc(ready, 1)

            def c_high_part(h, r):
                s = slice(HT * h, HT * (h + 1))
                act.wait_ge(hc_ready, R * h + r + 1)
                a.activation(xT_high[:, r, s], c_sb[:, r, s], ACT.Copy).then_inc(c_high_ready, 1)

            def cv_high_part(h, first, last):
                s = slice(HT * h, HT * (h + 1))
                for c in range(first, last):
                    act.wait_ge(gated_ready, CI * h + c + 1)
                    a.activation(cv_high[:, c, s], cv_sb[:, c, s], ACT.Copy).then_inc(cv_high_ready, 1)

            for h in range(2):
                s = slice(HT * h, HT * (h + 1))
                if h:
                    a.preload_act_table_set("natural_log_exp_and_others")
                dt_abs(h)
                if h:
                    log_term(h)
                for c in range(CI):
                    leave(h, XI0 + c, xi_sb[:, c, TAPS - 1 + HT * h:TAPS - 1 + HT * (h + 1)], xi_ready)
                if h == 0:
                    log_term(h)
                for r in range(R):
                    leave(h, B0 + r, b_sb[:, r, s], b_ready)
                if h == 0:
                    x_high(1)
                for r in range(R):
                    leave(h, C0 + r, c_sb[:, r, s], c_ready)
                decay(h)
                if h:
                    c_high_part(0, 0)
                    c_high_part(0, 1)
                for r in range(R):
                    for c in (2 * r, 2 * r + 1):
                        if (h, c) in POOL_CONV:
                            act.wait_ge(conv_pool_ready, POOL_CONV.index((h, c)) + 1)
                        else:
                            act.wait_ge(conv_ready, sum((h, c) not in POOL_CONV for h, c in CHUNKS[:CI * h + c + 1]))
                        a.activation(cv_sb[:, c, s], cv_sb[:, c, s], ACT.Silu).then_inc(xs_ready, 1)
                    for c in (2 * r, 2 * r + 1):
                        leave(h, Z0 + c, sz_sb[:, c, s], z_ready, ACT.Silu)
            cv_high_part(0, 0, 2)
            c_high_part(1, 0)
            cv_high_part(0, 2, CI)
            c_high_part(1, 1)

            def shared_hidden(first, last):
                for n in range(first, last):
                    m, h = n % SC, n // SC
                    act.wait_ge(up_s_done, n + 1)
                    dst = hs_sb[:, m, HT * h:HT * (h + 1)]
                    a.activation(dst, bank[4 + n % 4][:], ACT.Relu).then_inc(up_s_read, 1)
                    act.wait_ge(up_s_read, n + 1)
                    a.activation(dst, dst, ACT.Square).then_inc(hs_ready, 1)

            def score_half(h, b):
                act.wait_ge(logits_done, h + 1)
                a.activation(score[:, HI * h:HI * (h + 1), :], bank[b][:, 0:HI * E].rearrange("p (i e) -> p i e", e=E),
                             ACT.Sigmoid).then_inc(score_ready, 1)

            cv_high_part(1, 0, 1)
            root(var, group(0))
            root(var, group(1))
            cv_high_part(1, 1, 2)
            normalise(xl_sb, rows(xn_sb), 0, 3, ln_ready)
            cv_high_part(1, 2, CI)
            normalise(xl_sb, rows(xn_sb), 1, 4, ln_ready)
            root(var, group(0))
            root(var, group(1))
            normalise(xn_sb, rows(x_sb), 0, 5, xf_ready)
            normalise(xn_sb, rows(x_sb), 1, 6, xf_ready)
            root(var, group(2))
            normalise(xl_sb, rows(xn_sb), 2, 7, ln_ready)
            root(var, group(3))
            normalise(xl_sb, rows(xn_sb), 3, 8, ln_ready)
            root(var, group(2))
            normalise(xn_sb, rows(x_sb), 2, 9, xf_ready)
            root(var, group(3))
            normalise(xn_sb, rows(x_sb), 3, 10, xf_ready)
            a.preload_act_table(ACT.Sigmoid)
            score_half(0, 3)
            score_half(1, 2)
            shared_hidden(0, 2 * SC)
            def hidden_out(q, j):
                act.wait_ge(hT_done, j + 1)
                a.activation(hT[:, q % 2, :], bank[3][:, 0:P], ACT.Copy).then_inc(hT_ready, 1)

            def y_high(q, j):
                act.wait_ge(down_done, j + 1)
                act.wait_ge(gate_ready, j + 1)
                if not (type(j) is int and j < 2):
                    act.wait_ge(added, j - 1)
                a.activation(y_parts[:, q % 2, 0, :], bank[1][:, 0:D], ACT.Copy, scale=gate_s[:, q:q + 1])\
                    .then_inc(y_high_ready, 1)

            def expert_steps(it):
                for q in range(RING):
                    act.wait_ge(gT_done, it * RING + (q + 1))
                    a.activation(xgT[:, q % 2, :], bank[0][:, 0:D], ACT.Copy).then_inc(gT_ready, 1)
                    if q > 1 or type(it) is not int:
                        hidden_out((q - 2) % RING, it * RING + (q - 2))
                    if q > 2 or type(it) is not int:
                        y_high((q - 3) % RING, it * RING + (q - 3))
                    act.wait_ge(up_done, it * RING + (q + 1))
                    a.activation(hr[:, q % 2, :], bank[2][:, 0:EI], ACT.Relu).then_inc(relu_ready, 1)

            expert_steps(0)
            with act.Fori(1, PAIRS // RING) as it:
                expert_steps(it)
            for n in range(PAIRS, PAIRS + 3):
                if n < PAIRS + 2:
                    hidden_out((n - 2) % RING, n - 2)
                y_high((n - 3) % RING, n - 3)
            a.preload_act_table(ACT.Sqrt)
            root(var, group(0))
            for g in range(NGR):
                if g + 1 < NGR:
                    root(var, group(g + 1))
                normalise(xl_sb, total, g, 2 + 2 * NGR + g + 1, ln_ready)

        @block.vector
        def _(dve):
            v = nc.vector
            links = [0]

            def link(ins):
                links[0] += 1
                ins.then_inc(dve_link, 1)
                dve.wait_ge(dve_link, links[0])

            def stats(buf, g):
                tiles = range(GT * g, GT * (g + 1))
                for i in tiles:
                    ins = v.bn_stats(st[:, i, :], buf[i])
                link(ins)
                for i in tiles:
                    ins = v.bn_aggr(mv[:, i, :], st[:, i, :])
                link(ins)
                s = slice(GT * g, GT * (g + 1))
                v.tensor_scalar(var[:, s], mv[:, s, 1], LN_EPS, None, ALU.add).then_inc(var_ready, 1)

            roots = [0]

            def shift(g):
                s = slice(GT * g, GT * (g + 1))
                roots[0] += 1
                dve.wait_ge(std_ready, roots[0])
                link(v.reciprocal(rstd[:, s], std[:, s]))
                v.scalar_tensor_tensor(out=nmr[:, s], in0=mv[:, s, 0], scalar=-1.0, in1=rstd[:, s],
                                       op0=ALU.mult, op1=ALU.mult).then_inc(nmr_ready, 1)

            def step_size(h):
                s = slice(HT * h, HT * (h + 1))
                for r in range(R):
                    n = NPROJ * h + DT0 + r
                    dve.wait_ge(proj_done, n + 1)
                    v.tensor_scalar(dt_sb[:, r, s], bank[4 + n % 4][:], dt_bias[:, r:r + 1], 0.0, ALU.add, ALU.max)\
                        .then_inc(dt_read, 1)

            def norm_half(h):
                s = slice(HI * h, HI * (h + 1))
                for i in range(HI * h, HI * (h + 1)):
                    if i % GT == 0:
                        dve.wait_ge(x_loaded[i // GT], 16)
                    ins = v.bn_stats(st[:, i, :], x_sb[:, i, :])
                link(ins)
                for i in range(HI * h, HI * (h + 1)):
                    ins = v.bn_aggr(mv[:, i, :], st[:, i, :])
                link(ins)
                v.tensor_scalar(var[:, s], mv[:, s, 1], LN_EPS, None, ALU.add).then_inc(var_ready, 1)
                roots[0] += 1
                dve.wait_ge(std_ready, roots[0])
                link(v.reciprocal(rstd[:, s], std[:, s]))
                link(v.tensor_tensor(msq[:, s], rstd[:, s], rstd[:, s], ALU.mult))
                link(v.tensor_tensor(msq[:, s], msq[:, s], mv[:, s, 1], ALU.mult))
                v.tensor_scalar(msq[:, s], msq[:, s], RMS_EPS, None, ALU.add).then_inc(var_ready, 1)
                v.scalar_tensor_tensor(out=nmr[:, s], in0=mv[:, s, 0], scalar=-1.0, in1=rstd[:, s],
                                       op0=ALU.mult, op1=ALU.mult).then_inc(nmr_ready, 1)
                roots[0] += 1
                dve.wait_ge(std_ready, roots[0])
                link(v.reciprocal(rms[:, s], std[:, s]))
                v.tensor_tensor(both[:, s], rstd[:, s], rms[:, s], ALU.mult)
                dve.wait_ge(nmr_ready, h + 1)
                link(v.tensor_tensor(nmb[:, s], nmr[:, s], rms[:, s], ALU.mult))
                if h:
                    step_size(0)
                for i in range(HI * h, HI * (h + 1)):
                    v.tensor_scalar(xn_sb[:, i, :], x_sb[:, i, :], both[:, i:i + 1], nmb[:, i:i + 1], ALU.mult, ALU.add)\
                        .then_inc(xn_ready, 1)

            def x_low(h):
                for k in range(KD):
                    dve.wait_ge(xT_high_ready, KD * h + k + 1)
                    t = slice(HT * h, HT * (h + 1))
                    v.scalar_tensor_tensor(out=xT_low[:, k, t], in0=bank[KD * h + k][:], scalar=w_norm[:, k:k + 1],
                                           in1=xT_high[:, k, t].bitcast(F32), op0=ALU.mult, op1=ALU.subtract)\
                        .then_inc(xT_low_ready, 1)

            norm_half(0)
            dve.wait_ge(ch_loaded, 16)
            x_low(0)
            norm_half(1)

            def convolve(h, c):
                s = slice(HT * h, HT * (h + 1))
                dve.wait_ge(xi_ready, CI * h + c + 1)
                link(v.tensor_scalar(cv_sb[:, c, s], xi_sb[:, c, HT * h:HT * h + HT], taps[:, c, 0:1], None, ALU.mult))
                for k in range(1, TAPS):
                    ins = v.scalar_tensor_tensor(out=cv_sb[:, c, s], in0=xi_sb[:, c, HT * h + k:HT * h + k + HT],
                                                 scalar=taps[:, c, k:k + 1], in1=cv_sb[:, c, s],
                                                 op0=ALU.mult, op1=ALU.add)
                    if k < TAPS - 1:
                        link(ins)
                    else:
                        ins.then_inc(conv_ready, 1)

            def scan(h, r):
                s = slice(HT * h, HT * (h + 1))
                dve.wait_ge(dt_ready, R * h + r + 1)
                dve.wait_ge(da_ready, R * h + r + 1)
                dve.wait_ge(mean_done, R * h + r + 1)
                v.tensor_tensor(dt_sb[:, r, s], bank[R * h + r][:], dt_sb[:, r, s], ALU.mult).then_inc(mean_read, 1)
                dve.wait_ge(mean_read, R * h + r + 1)
                dve.wait_ge(b_ready, R * h + r + 1)
                link(v.tensor_tensor(b_sb[:, r, s], dt_sb[:, r, s], b_sb[:, r, s], ALU.mult))
                first = 0.0 if h == 0 else sp_sb[:, r, HT - 1:HT]
                link(v.tensor_tensor_scan(sp_sb[:, r, s], da_sb[:, r, s], b_sb[:, r, s], first, ALU.mult, ALU.add))
                dve.wait_ge(c_ready, R * h + r + 1)
                v.tensor_tensor(c_sb[:, r, s], sp_sb[:, r, s], c_sb[:, r, s], ALU.mult).then_inc(hc_ready, 1)

            def c_low_part(h, r):
                s = slice(HT * h, HT * (h + 1))
                dve.wait_ge(c_high_ready, R * h + r + 1)
                v.tensor_tensor(xT_low[:, r, s], c_sb[:, r, s], xT_high[:, r, s].bitcast(F32), ALU.subtract)\
                    .then_inc(c_low_ready, 1)

            def finish_dt(h):
                s = slice(HT * h, HT * (h + 1))
                for r in range(R):
                    dve.wait_ge(sp_ready, R * h + r + 1)
                    dve.wait_ge(dt_read, R * h + r + 1)
                    v.tensor_tensor(dt_sb[:, r, s], dt_sb[:, r, s], sp_sb[:, r, s], ALU.add).then_inc(dt_ready, 1)

            dve.wait_ge(pads_zeroed, 1)
            convolve(0, 0)
            convolve(0, 1)
            finish_dt(0)
            x_low(1)
            convolve(0, 2)
            convolve(0, 3)
            step_size(1)
            scan(0, 0)
            convolve(1, 0)
            finish_dt(1)
            scan(0, 1)
            convolve(1, 1)
            c_low_part(0, 0)
            c_low_part(0, 1)
            convolve(1, 2)

            def gate(h, first, last):
                s = slice(HT * h, HT * (h + 1))
                for c in range(first, last):
                    dve.wait_ge(h2i_done, CI * h + c + 1)
                    dve.wait_ge(z_ready, CI * h + c + 1)
                    v.tensor_tensor(cv_sb[:, c, s], bank[H2I[h][c]][:], sz_sb[:, c, s], ALU.mult).then_inc(gated_ready, 1)

            def mixed(g):
                for i in range(GT * g, GT * (g + 1)):
                    dve.wait_ge(mix_done, i + 1)
                    v.tensor_tensor(xn_sb[:, i, :], bank[i % HI][:, 0:D], xl_sb[:, i, :], ALU.add)\
                        .then_inc(mix_read, 1)

            def mixed_stats(g):
                dve.wait_ge(mix_read, GT * (g + 1))
                stats(rows(xn_sb), g)

            def x1_stats(g):
                dve.wait_ge(x1_ready, g + 1)
                stats(rows(x_sb), g)

            def mixed_low(c):
                s = slice(HT, T)
                dve.wait_ge(cv_high_ready, CI + c + 1)
                v.tensor_tensor(cv_low[:, c, s], cv_sb[:, c, s], cv_high[:, c, s].bitcast(F32), ALU.subtract)\
                    .then_inc(cv_low_late, 1)

            def leave_transposed(h, first):
                for k in range(KD):
                    dve.wait_ge(xfT_in_psum, KD * h + k + 1)
                    v.tensor_copy(xT_sb[:, k, HT * h:HT * (h + 1)], bank[first + k][:]).then_inc(xfT_ready, 1)

            def layer_norms_first():
                mixed(0)
                mixed(1)
                mixed_stats(0)
                gate(1, 0, 1)
                mixed_stats(1)
                gate(1, 1, 2)
                shift(0)
                gate(1, 2, 3)
                shift(1)
                gate(1, 3, CI)
                mixed_low(2)
                mixed_low(3)
                x1_stats(0)
                x1_stats(1)
                shift(0)
                shift(1)

            def layer_norms_second():
                mixed(2)
                mixed_stats(2)
                mixed(3)
                shift(2)
                mixed_stats(3)
                shift(3)
                leave_transposed(0, 4)
                x1_stats(2)
                shift(2)
                x1_stats(3)
                shift(3)
                leave_transposed(1, 0)

            def flat(ap):
                return ap.rearrange("p i e -> p (i e)")

            def merge(first, low_first, last, low_last, hi, tmp, lo, sec):
                v.tensor_tensor(hi, first, last, ALU.max)
                v.tensor_tensor(tmp, first, last, ALU.min)
                link(v.tensor_tensor(lo, low_first, low_last, ALU.max))
                link(v.tensor_tensor(sec, tmp, lo, ALU.max))

            def score_groups(h):
                s = slice(HI * h, HI * (h + 1))
                dve.wait_ge(score_ready, h + 1)
                link(v.tensor_tensor(biased[:, s, :], score[:, s, :], eb_sb[:].unsqueeze(1).to_broadcast([P, HI, E]),
                                     ALU.add))
                grp = flat(biased[:, s, :]).rearrange("p (g m) -> p g m", m=GE)
                v.tensor_tensor(t4[0], grp[:, :, 0:4], grp[:, :, 4:8], ALU.max)
                link(v.tensor_tensor(t4[1], grp[:, :, 0:4], grp[:, :, 4:8], ALU.min))
                merge(t4[0][:, :, 0:2], t4[1][:, :, 0:2], t4[0][:, :, 2:4], t4[1][:, :, 2:4],
                      t2[0], t2[1], t2[2], t2[3])
                merge(t2[0][:, :, 0], t2[3][:, :, 0], t2[0][:, :, 1], t2[3][:, :, 1], g1[0], g1[1], g1[2], g1[3])
                link(v.tensor_tensor(flat(gs[:, s, :]), g1[0], g1[3], ALU.add))

            def route():
                for i in range(NT):
                    ins = v.max(gtop[:, i, :], gs[:, i, :])
                link(ins)
                link(v.memset(gtop[:, :, TOPG:NG], BIG))
                for i in range(NT):
                    ins = v.match_replace(out=gleft[:, i, :], in_to_replace=gtop[:, i, :], in_values=gs[:, i, :],
                                          imm_value=-2.0 * BIG)
                link(ins)
                link(v.tensor_tensor(gmask, gleft, gs, ALU.is_equal))
                v.memset(masked[:, :, E:E + 2], BIG)
                link(v.scalar_tensor_tensor(out=masked[:, :, 0:E].rearrange("p i (g m) -> p i g m", m=GE),
                                            in0=gmask.unsqueeze(3).to_broadcast([P, NT, NG, GE]), scalar=-BIG,
                                            in1=biased.rearrange("p i (g m) -> p i g m", m=GE),
                                            op0=ALU.mult, op1=ALU.add))
                for i in range(NT):
                    ins = v.max(top8[:, i, :], masked[:, i, :])
                link(ins)
                for i in range(NT):
                    ins = v.match_replace(out=masked2[:, i, :], in_to_replace=top8[:, i, :], in_values=masked[:, i, :],
                                          imm_value=-2.0 * BIG)
                link(ins)
                v.tensor_tensor(sel_b[:], masked[:, :, 0:E], masked2[:, :, 0:E], ALU.not_equal)\
                    .then_inc(sel_ready, 1)
                dve.wait_ge(sel_ready, 1)
                link(v.tensor_tensor(picked, score, sel_b[:], ALU.mult))
                link(v.tensor_reduce(wsum[:], picked, AX_X, ALU.add))

            gate(0, 0, 2)
            scan(1, 0)
            gate(0, 2, CI)
            c_low_part(1, 0)
            scan(1, 1)
            c_low_part(1, 1)
            dve.wait_ge(ln_ready, NT)
            layer_norms_first()
            layer_norms_second()
            dve.wait_ge(eb_loaded, 16)
            score_groups(0)
            score_groups(1)
            route()
            link(v.tensor_scalar(wsum[:], wsum[:], 1e-20, None, ALU.add))
            link(v.reciprocal(norm[:], wsum[:]))
            v.tensor_scalar(norm[:], norm[:], SCALE, None, ALU.mult).then_inc(norm_ready, 1)
            dve.wait_ge(pos_done, 1)
            pos = bank[1][:].rearrange("p (i e) -> p i e", e=E)
            link(v.scalar_tensor_tensor(out=biased, in0=pos, scalar=float(CAP), in1=sel_b[:], op0=ALU.is_lt, op1=ALU.mult))
            keep_h = biased.rearrange("p (h i) e -> p i h e", h=2)
            key_h = cst[:, C_KEY:C_KEY + NT].rearrange("p (h i) -> p i h", h=2).unsqueeze(3).to_broadcast([P, HI, 2, E])
            v.tensor_tensor(keyt, keep_h, key_h, ALU.mult).then_inc(keyt_ready, 1)
            dve.wait_ge(keys_in_psum, 1)
            src = bank[3][:]
            for n in range(CAP // 8):
                link(v.max(lists[:, 8 * n:8 * n + 8], src))
                if n < CAP // 8 - 1:
                    link(v.match_replace(out=work, in_to_replace=lists[:, 8 * n:8 * n + 8], in_values=src, imm_value=0.0))
                    src = work
            for b in range(2):
                par = cst[:, C_PAR + b:C_PAR + b + 1]
                v.tensor_scalar(ltab[0:E, b, :], lists[0:E, :], par[0:E], None, ALU.mult)
                ins = v.tensor_scalar(ltab[E:P, b, :], lists[E:P, ::-1], par[E:P], None, ALU.mult)
            ins.then_inc(ltab_ready, 1)
            dve.wait_ge(tokens_done, 1)
            link(v.tensor_scalar(tokf, bank[3][:, 0:PAIRS], -1.0, float(T), ALU.mult, ALU.add))
            v.tensor_scalar(tok_u[:], tokf, float(T - 1), None, ALU.min).then_inc(tok_ready, 1)

            def y_low(q, j):
                dve.wait_ge(y_high_ready, j + 1)
                v.scalar_tensor_tensor(out=y_parts[:, q % 2, 1, :], in0=bank[1][:, 0:D], scalar=gate_s[:, q:q + 1],
                                       in1=y_parts[:, q % 2, 0, :].bitcast(F32), op0=ALU.mult, op1=ALU.subtract)\
                    .then_inc(y_low_ready, 1)

            def expert_steps(it):
                for q in range(RING):
                    if q > 2 or type(it) is not int:
                        y_low((q - 3) % RING, it * RING + (q - 3))
                    dve.wait_ge(gathered[q], it * 16 + 16)
                    v.scalar_tensor_tensor(out=gate2[:, q, :], in0=xg[:, q, bass.ds(it * 2 * RING + (D + 2 * q), 2)], scalar=1.0,
                                           in1=cst[:, C_SIDE:C_SIDE + 2], op0=ALU.mult, op1=ALU.mult,
                                           accum_out=gate_s[:, q:q + 1]).then_inc(gate_ready, 1)
                    if not (type(it) is int and q < HOTS):
                        dve.wait_ge(added, it * RING + (q - HOTS + 1))
                    v.tensor_scalar(hot[:, q % HOTS, :], token_no, tokf[:, bass.ds(it * RING + q, 1)], None,
                                    ALU.is_equal).then_inc(hot_ready, 1)
                    dve.wait_ge(relu_ready, it * RING + (q + 1))
                    v.tensor_tensor(hx[:, q % 2, :], hr[:, q % 2, :], bank[2][:, 0:EI], ALU.mult)\
                        .then_inc(hid_ready, 1)

            dve.wait_ge(token_no_ready, 1)
            expert_steps(0)
            with dve.Fori(1, PAIRS // RING) as it:
                expert_steps(it)
            for n in range(PAIRS - 3, PAIRS):
                y_low(n % RING, n)
            dve.wait_ge(sum_done, 1)
            stats(total, 0)
            for g in range(NGR):
                if g + 1 < NGR:
                    dve.wait_ge(sum_done, g + 2)
                    stats(total, g + 1)
                shift(g)
            for i in range(GT * (NGR - 1), NT):
                dve.wait_ge(ln_ready, 2 * NT + i + 1)
                v.tensor_tensor(x_sb[:, i, :], x_sb[:, i, :], xl_sb[:, i, :], ALU.add).then_inc(fin_last, 1)

        @block.tensor
        def _(pe):
            t = nc.tensor
            pe.wait_ge(consts_b, 1)
            def keep_warm(products):
                for n in range(products):
                    t.matmul(bank[7][:].rearrange("p (i c) -> p i c", c=P), ones_b[:],
                             ones_b[:].unsqueeze(1).to_broadcast([P, 4, P]), start=True, stop=True)

            keep_warm(WARM)
            pe.wait_ge(cst_loaded, 16)
            def transpose_x(h):
                pe.wait_ge(xn_ready, HI * (h + 1))
                for k in range(KD):
                    for i in range(HI):
                        ins = t.transpose(bank[KD * h + k][:, P * i:P * (i + 1)],
                                          xn_sb[:, HI * h + i, P * k:P * (k + 1)], ident)
                    ins.then_inc(xT_in_psum, 1)

            def wait_left(n):
                h, m = divmod(n, NPROJ)
                for first, count, left in ((Z0, CI, z_ready), (C0, R, c_ready), (B0, R, b_ready),
                                           (XI0, CI, xi_ready), (DT0, R, abs_ready)):
                    if m >= first:
                        pe.wait_ge(left, count * h + m - first + 1)
                        return

            def project(h, first, last):
                for m in range(first, last):
                    n = NPROJ * h + m
                    if n >= 4:
                        wait_left(n - 4)
                    pe.wait_ge(w_low_ready, m // WP + 1)
                    for k in range(KD):
                        mm, tt = slice(P * m, P * (m + 1)), slice(HT * h, HT * (h + 1))
                        t.matmul(bank[4 + n % 4][:], w_high[:, k, mm], xT_high[:, k, tt], start=(k == 0), stop=False)
                        t.matmul(bank[4 + n % 4][:], w_high[:, k, mm], xT_low[:, k, tt], start=False, stop=False)
                        ins = t.matmul(bank[4 + n % 4][:], w_low[:, k, mm], xT_high[:, k, tt], start=False,
                                       stop=(k == KD - 1))
                    ins.then_inc(proj_done, 1)

            def mean(h, r):
                for q in range(2):
                    c = 2 * r + q
                    pe.wait_ge(xs_ready, CI * h + c + 1)
                    ins = t.matmul(bank[R * h + r][P // 2 * q:P // 2 * (q + 1), :], cst[:, C_SEL:C_SEL + P // 2],
                                   cv_sb[:, c, HT * h:HT * (h + 1)], start=True, stop=True)
                ins.then_inc(mean_done, 1)

            transpose_x(0)
            pe.wait_ge(xT_low_ready, KD)
            project(0, 0, XI0 + CI)
            transpose_x(1)
            project(0, XI0 + CI, NPROJ)
            pe.wait_ge(xT_low_ready, 2 * KD)
            mean(0, 0)
            project(1, 0, XI0)
            mean(0, 1)
            project(1, XI0, NPROJ)

            def transpose_group(g, first):
                pe.wait_ge(xf_ready, GT * (g + 1))
                for k in range(KD):
                    for i in range(GT * g, GT * (g + 1)):
                        ins = t.transpose(bank[first + k][:, P * (i % HI):P * (i % HI + 1)],
                                          xn_sb[:, i, P * k:P * (k + 1)], ident)
                    if g % 2:
                        ins.then_inc(xfT_in_psum, 1)

            def score_experts(h, b):
                pe.wait_ge(xfT_ready, KD * (h + 1))
                for i in range(HI * h, HI * (h + 1)):
                    for k in range(KD):
                        ins = t.matmul(bank[b][:, E * (i % HI):E * (i % HI + 1)], xT_sb[:, k, P * i:P * (i + 1)],
                                       gw_sb[:, k, :], start=(k == 0), stop=(k == KD - 1))
                ins.then_inc(logits_done, 1)

            def shared_up(first, last):
                for n in range(first, last):
                    m, h = n % SC, n // SC
                    if n >= 4:
                        pe.wait_ge(up_s_read, n - 3)
                    for k in range(KD):
                        ins = t.matmul(bank[4 + n % 4][:], su_sb[:, k, P * m:P * (m + 1)],
                                       xT_sb[:, k, HT * h:HT * (h + 1)], start=(k == 0), stop=(k == KD - 1))
                    ins.then_inc(up_s_done, 1)

            def shared_down(first, last, chunks=range(SC)):
                for i in range(first, last):
                    pe.wait_ge(hs_ready, SC * (i // HI + 1))
                    for m in chunks:
                        t.matmul(total[i], hs_sb[:, m, P * i:P * (i + 1)], sd_sb[:, m, :],
                                 start=(m == 0 and i % 2 == 0), stop=False)

            def spread(h, first, last):
                pe.wait_ge(c_low_ready, R * (h + 1))
                for c in range(first, last):
                    b = H2I[h][c]
                    if h and b in H2I[0]:
                        pe.wait_ge(gated_ready, H2I[0].index(b) + 1)
                    elif b >= 4:
                        wait_left(2 * NPROJ - CI + b - 4)
                    for r in range(R):
                        cc, tt = slice(P * c, P * (c + 1)), slice(HT * h, HT * (h + 1))
                        t.matmul(bank[b][:], wh_high[:, r, cc], xT_high[:, r, tt], start=(r == 0), stop=False)
                        t.matmul(bank[b][:], wh_high[:, r, cc], xT_low[:, r, tt], start=False, stop=False)
                        ins = t.matmul(bank[b][:], wh_low[:, r, cc], xT_high[:, r, tt],
                                       start=False, stop=(r == R - 1))
                    ins.then_inc(h2i_done, 1)

            def mix(h):
                for c in range(CI):
                    if h and c >= 2:
                        pe.wait_ge(cv_low_late, c - 1)
                    else:
                        pe.wait_ge(cv_low_ready, CI * h + c + 1)
                    for i in range(HI * h, HI * (h + 1)):
                        if c == 0 and h:
                            pe.wait_ge(mix_read, i - HI + 1)
                        elif c == 0 and i >= R:
                            pe.wait_ge(mean_read, i + 1)
                        elif c == 0:
                            pe.wait_ge(gated_ready, H2I[0].index(i) + 1)
                        o, tt = bank[i % HI][:, 0:D], slice(P * i, P * (i + 1))
                        t.matmul(o, cv_high[:, c, tt], wo_high[:, c, :], start=(c == 0), stop=False)
                        t.matmul(o, cv_high[:, c, tt], wo_low[:, c, :], start=False, stop=False)
                        ins = t.matmul(o, cv_low[:, c, tt], wo_high[:, c, :], start=False, stop=(c == CI - 1))
                        if c == CI - 1:
                            ins.then_inc(mix_done, 1)

            pe.wait_ge(mixw_ready, 1)
            spread(0, 0, 2)
            mean(1, 0)
            mean(1, 1)
            spread(0, 2, CI)
            pe.wait_ge(mixw_ready, 2)
            mix(0)
            spread(1, 0, CI)
            mix(1)
            pe.wait_ge(gated_ready, 2 * CI)
            transpose_group(0, 4)
            transpose_group(1, 4)
            keep_warm(10)
            pe.wait_ge(gw_loaded, 16)
            pe.wait_ge(mix_read, NT)
            score_experts(0, 3)
            transpose_group(2, 0)
            transpose_group(3, 0)
            keep_warm(3)
            score_experts(1, 2)
            pe.wait_ge(su_loaded, 16)
            shared_up(0, 4)
            pe.wait_ge(consts_b, 2)
            pe.wait_ge(sel_ready, 1)
            t.matmul(bank[1][:], tri_b[:], sel_b[:].rearrange("p i e -> p (i e)"), start=True, stop=False)
            for i in range(NT - 1):
                rest = NT - 1 - i
                ins = t.matmul(bank[1][:, E * (i + 1):E * NT].rearrange("p (i e) -> p i e", e=E), ones_b[:],
                         sel_b[:, i, :].unsqueeze(1).to_broadcast([P, rest, E]), start=False, stop=(rest == 1))
            ins.then_inc(pos_done, 1)
            shared_up(4, 5)
            pe.wait_ge(keyt_ready, 1)
            for i in range(HI):
                ins = t.transpose(bank[3][:, P * i:P * (i + 1)], keyt[:, i, :, :].rearrange("p h e -> p (h e)"), ident)
            ins.then_inc(keys_in_psum, 1)

            shared_up(5, 2 * SC)
            pe.wait_ge(sd_loaded, 16)
            pe.wait_ge(up_s_read, 2 * SC)
            shared_down(0, NT - 4)
            pe.wait_ge(ltab_ready, 1)
            t.matmul(bank[3][:, 0:PAIRS], ltab.rearrange("p b c -> p (b c)"), cst[:, C_PAIR:C_PAIR + PAIRS],
                     start=True, stop=True).then_inc(tokens_done, 1)
            shared_down(NT - 4, NT - 2)
            def transpose_slots(it, q):
                pe.wait_ge(gathered[q], it * 16 + 16)
                if not (type(it) is int and it * RING + q < 1):
                    pe.wait_ge(gT_ready, it * RING + q)
                for k in range(KD):
                    ins = t.transpose(bank[0][:, P * k:P * (k + 1)], xg[:, q, P * k:P * (k + 1)], ident)
                ins.then_inc(gT_done, 1)

            def up(it, q):
                s = q % 2
                pe.wait_ge(ring_loaded[q], it * 16 + 16)
                pe.wait_ge(gT_ready, it * RING + (q + 1))
                if not (type(it) is int and it * RING + q < 1):
                    pe.wait_ge(hid_ready, it * RING + q)
                for k in range(KD):
                    for b in range(2):
                        ins = t.matmul(bank[2][CAP * b:CAP * (b + 1), 0:EI],
                                       xgT[:, s, P * k + CAP * b:P * k + CAP * (b + 1)],
                                       ring[:, q, b, P * k:P * (k + 1)], start=(k == 0), stop=(k == KD - 1))
                ins.then_inc(up_done, 1)

            def turn(q, j):
                pe.wait_ge(hid_ready, j + 1)
                if not (type(j) is int and j < 1):
                    pe.wait_ge(hT_ready, j)
                t.transpose(bank[3][:, 0:P], hx[:, q % 2, :], ident).then_inc(hT_done, 1)

            def down(q, j):
                s = q % 2
                pe.wait_ge(hT_ready, j + 1)
                if not (type(j) is int and j < 1):
                    pe.wait_ge(y_low_ready, j)
                for b in range(2):
                    ins = t.matmul(bank[1][CAP * b:CAP * (b + 1), 0:D], hT[:, s, CAP * b:CAP * (b + 1)],
                                   ring[:, q, b, D:2 * D], start=True, stop=True)
                ins.then_inc(down_done, 1)

            def add(q, j):
                pe.wait_ge(hot_ready, j + 1)
                pe.wait_ge(y_low_ready, j + 1)
                for i in range(NT):
                    for part in range(2):
                        ins = t.matmul(total[i], hot[:, q % HOTS, P * i:P * (i + 1)], y_parts[:, q % 2, part, :],
                                       start=False, stop=False)
                ins.then_inc(added, 1)

            def add_last():
                pe.wait_ge(hot_ready, PAIRS)
                pe.wait_ge(y_low_ready, PAIRS)
                for i in range(NT):
                    for q in (RING - 2, RING - 1):
                        for part in range(2):
                            end = i % 2 == 1 and q == RING - 1 and part == 1
                            ins = t.matmul(total[i], hot[:, q % HOTS, P * i:P * (i + 1)], y_parts[:, q % 2, part, :],
                                           start=False, stop=end)
                    if i % 2:
                        ins.then_inc(sum_done, 1)

            def expert_steps(it, last=False):
                for q in range(RING):
                    if q + 1 < RING:
                        transpose_slots(it, q + 1)
                    elif not last:
                        transpose_slots(it + 1, 0)
                    up(it, q)
                    if type(it) is int and it == 0 and q < 4:
                        i, m = NT - 2 + q // 2, SC // 2 * (q % 2)
                        shared_down(i, i + 1, range(m, m + SC // 2))
                    for lag, step in ((1, turn), (2, down), (3, add)):
                        if q >= lag or type(it) is not int or it:
                            step((q - lag) % RING, it * RING + (q - lag))

            transpose_slots(0, 0)
            expert_steps(0)
            with pe.Fori(1, PAIRS // RING - 1) as it:
                expert_steps(it)
            expert_steps(PAIRS // RING - 1, last=True)
            turn(RING - 1, PAIRS - 1)
            down(RING - 2, PAIRS - 2)
            add(RING - 3, PAIRS - 3)
            down(RING - 1, PAIRS - 1)
            add_last()

def kernel(L0_attn_x, L0_attn_w_norm, L0_attn_W_in, L0_attn_w_conv, L0_attn_dt_bias, L0_attn_A_log, L0_attn_W_h2i,
           L0_attn_W_out, L0_ffn_gate_w, L0_ffn_e_bias, L0_ffn_w1, L0_ffn_w2, L0_ffn_shared_up_w,
           L0_ffn_shared_down_w):
    import concourse.bacc as bacc
    from concourse.bass_utils import run_bass_kernel_spmd

    W = np.asarray(L0_attn_W_in)
    o = 2 * DI + H
    rows = [np.repeat(W[2 * DI:o], N, axis=0), W[DI:2 * DI], W[o:o + HN], W[o + HN:], W[:DI]]
    w_in = np.concatenate(rows, axis=0).T

    def by_partition(a):
        return np.asarray(a).reshape(-1, P).T

    chan = np.concatenate([
        np.asarray(L0_attn_w_conv).reshape(CI, P, TAPS).transpose(1, 0, 2).reshape(P, CI * TAPS),
        by_partition(L0_attn_w_norm),
        by_partition(np.repeat(np.asarray(L0_attn_dt_bias), N)),
        by_partition(np.repeat(np.asarray(L0_attn_A_log), N))], axis=1)
    w1 = np.asarray(L0_ffn_w1).reshape(PAIRS, 2, EI, KD, P).transpose(0, 4, 1, 3, 2).reshape(PAIRS, P, 2, KD * EI)
    w2 = np.asarray(L0_ffn_w2).reshape(PAIRS, 2, D, EI).transpose(0, 3, 1, 2)
    arrays = {
        "x": np.asarray(L0_attn_x),
        "consts": constants(),
        "w_in": w_in,
        "chan": chan,
        "w_h2i": np.repeat(np.asarray(L0_attn_W_h2i).T, N, axis=0),
        "w_out": np.asarray(L0_attn_W_out).T,
        "gate_w": np.asarray(L0_ffn_gate_w).T,
        "e_bias": np.tile(np.asarray(L0_ffn_e_bias)[None, :], (P, 1)),
        "w_exp": np.concatenate([w1, w2], axis=3).reshape(PAIRS, P, 4 * D),
        "w_su": np.asarray(L0_ffn_shared_up_w).T,
        "w_sd": np.asarray(L0_ffn_shared_down_w).T,
    }
    arrays = {n: np.ascontiguousarray(a) for n, a in arrays.items()}
    nc = bacc.Bacc("TRN2", target_bir_lowering=False, num_devices=1)
    aps = [nc.dram_tensor(f"in_{n}", a.shape, mybir.dt.from_np(a.dtype), kind="ExternalInput").ap()
           for n, a in arrays.items()]
    out = nc.dram_tensor("out_x", (1, T, D), F32, kind="ExternalOutput").ap()
    program(nc, *aps, out)
    r = run_bass_kernel_spmd(nc, [{f"in_{n}": a for n, a in arrays.items()}], core_ids=[0])
    return r.results[0]["out_x"]
```
